# Optimizing a Trainium2 kernel written in Bass

```python
import numpy as np
import jax
import jax.numpy as jnp

def _softmax(x, axis=-1):
    return jax.nn.softmax(x, axis=axis)

def _gelu(x):
    return jax.nn.gelu(x, approximate=True)

def _silu(x):
    return jax.nn.silu(x)

def _sigmoid(x):
    return jax.nn.sigmoid(x)

def _layernorm(x, axis=-1, eps=1e-05):
    m = jnp.mean(x, axis=axis, keepdims=True)
    v = jnp.var(x, axis=axis, keepdims=True)
    return (x - m) / jnp.sqrt(v + eps)

def _scatter_add(tgt, idx, src, axis=0):
    return tgt.at[idx].add(src)

def _segment_sum(src, seg, n):
    return jax.ops.segment_sum(src, seg, n)
kernel_name = 'mk_decoder_postln_d1_seqx_r2_33f22c'

def setup_inputs(seed: int=0):
    np.random.seed(seed)
    _w = jnp.asarray

    def _rec_inputs():
        import jax
        import jax.numpy as jnp
        _rk = jax.random.key(seed)
        x = -0.0002928 + 1 * jax.random.normal(jax.random.fold_in(_rk, 1), (8, 100, 512), jnp.float32)
        _lenS = 100 - jax.random.randint(jax.random.fold_in(_rk, 7), (8,), 0, max(1, 100 // 4) + 1, jnp.int32)
        _lenS2 = 722 - jax.random.randint(jax.random.fold_in(_rk, 8), (8,), 0, max(1, 722 // 4) + 1, jnp.int32)
        _ctx_1024P = jax.random.normal(jax.random.fold_in(_rk, 11), (8, 16, 512), jnp.float32)
        _ctx_1024c = jax.random.dirichlet(jax.random.fold_in(_rk, 511), 0.3 * jnp.ones((16,), jnp.float32), (8, 722))
        _ctx_1024t = jnp.einsum('bsk,bkd->bsd', _ctx_1024c, _ctx_1024P)
        _ctx_1024t = _ctx_1024t * jax.lax.rsqrt(jnp.mean(jnp.square(_ctx_1024t)) + 1e-12) * 0.953939
        ctx_1024 = -1.39393e-06 + 0.999914 * (_ctx_1024t + 0.3 * jax.random.normal(jax.random.fold_in(_rk, 611), (8, 722, 512), jnp.float32))
        return (x, ctx_1024)
    x, ctx_1024 = _rec_inputs()

    def _L0_attn_setup():
        import jax, jax.numpy as jnp
        import numpy as np
        L, B, E, H = (1024, 4, 512, 8)
        D1 = 2 * E
        EPS = 1e-08

        def _toeplitz_mix(v, pos, zero, neg):
            b, h, n, d = v.shape
            m = 2 * n
            a = jnp.concatenate([zero, pos[:, :n - 1], jnp.zeros((h, 1), v.dtype), neg[:, :n - 1][:, ::-1]], axis=-1)
            af = jnp.fft.rfft(a, n=m, axis=-1)
            vf = jnp.fft.rfft(v, n=m, axis=-2)
            y = jnp.fft.irfft(af[None, :, :, None] * vf, n=m, axis=-2)
            return y[:, :, :n, :]
        key = jax.random.key(seed)
        ks = jax.random.split(key, 12)
        std = 0.02
        return {'query': jax.random.normal(ks[0], (L, B, E), jnp.float32), 'key': jax.random.normal(ks[1], (L, B, E), jnp.float32), 'value': jax.random.normal(ks[2], (L, B, E), jnp.float32), 'u_w': jax.random.normal(ks[3], (D1, E), jnp.float32) * std, 'u_b': jax.random.normal(ks[4], (D1,), jnp.float32) * std, 'v_w': jax.random.normal(ks[5], (D1, E), jnp.float32) * std, 'v_b': jax.random.normal(ks[6], (D1,), jnp.float32) * std, 'o_w': jax.random.normal(ks[7], (E, D1), jnp.float32) * std, 'o_b': jax.random.normal(ks[8], (E,), jnp.float32) * std, 'pos': jax.random.normal(ks[9], (H, L - 1), jnp.float32) * std, 'zero': jax.random.normal(ks[10], (H, 1), jnp.float32) * std, 'neg': jax.random.normal(ks[11], (H, L - 1), jnp.float32) * std}
    _L0_attn_all = _L0_attn_setup()
    _L0_attn_in = {k: v for k, v in _L0_attn_all.items() if k in ('key', 'value', 'u_w', 'u_b', 'v_w', 'v_b', 'o_w', 'o_b', 'pos', 'zero', 'neg')}
    del _L0_attn_all

    def _L0_xattn_setup():
        import jax, jax.numpy as jnp
        import numpy as np
        import math
        D_MODEL = 512
        N_HEADS = 16
        key = jax.random.key(seed)
        ks = jax.random.split(key, 11)
        N, L, S = (2, 1024, 1024)
        d = D_MODEL
        s = 1.0 / math.sqrt(d)
        return {'queries': jax.random.normal(ks[0], (N, L, d), dtype=jnp.float32), 'keys': jax.random.normal(ks[1], (N, S, d), dtype=jnp.float32), 'values': jax.random.normal(ks[2], (N, S, d), dtype=jnp.float32), 'Wq': jax.random.normal(ks[3], (d, d), dtype=jnp.float32) * s, 'bq': jax.random.normal(ks[4], (d,), dtype=jnp.float32) * s, 'Wk': jax.random.normal(ks[5], (d, d), dtype=jnp.float32) * s, 'bk': jax.random.normal(ks[6], (d,), dtype=jnp.float32) * s, 'Wv': jax.random.normal(ks[7], (d, d), dtype=jnp.float32) * s, 'bv': jax.random.normal(ks[8], (d,), dtype=jnp.float32) * s, 'Wo': jax.random.normal(ks[9], (d, d), dtype=jnp.float32) * s, 'bo': jax.random.normal(ks[10], (d,), dtype=jnp.float32) * s}
    _L0_xattn_all = _L0_xattn_setup()
    _L0_xattn_in = {k: v for k, v in _L0_xattn_all.items() if k in ('Wq', 'bq', 'Wk', 'bk', 'Wv', 'bv', 'Wo', 'bo')}
    del _L0_xattn_all

    def _L0_ffn_setup():
        import jax, jax.numpy as jnp
        import numpy as np
        B, T, D = (2, 1024, 512)
        E, DFF, TOPK = (8, 2048, 2)
        TEMPERATURE = 1.0
        key = jax.random.key(seed)
        k_x, k_w1, k_w2, k_r = jax.random.split(key, 4)
        x = jax.random.normal(k_x, (B, T, D), dtype=jnp.float32)
        W1 = jax.random.normal(k_w1, (E, DFF, D), dtype=jnp.float32) * 0.02
        W2 = jax.random.normal(k_w2, (E, D, DFF), dtype=jnp.float32) * 0.02
        Wr = jax.random.normal(k_r, (E, D), dtype=jnp.float32) * 0.02
        return {'x': x, 'W1': W1, 'W2': W2, 'Wr': Wr}
    _L0_ffn_all = _L0_ffn_setup()
    _L0_ffn_in = {k: v for k, v in _L0_ffn_all.items() if k in ('W1', 'W2', 'Wr')}
    del _L0_ffn_all
    return {'x': x, 'ctx_1024': ctx_1024, 'L0_attn_key': _L0_attn_in['key'], 'L0_attn_value': _L0_attn_in['value'], 'L0_attn_u_w': _L0_attn_in['u_w'], 'L0_attn_u_b': _L0_attn_in['u_b'], 'L0_attn_v_w': _L0_attn_in['v_w'], 'L0_attn_v_b': _L0_attn_in['v_b'], 'L0_attn_o_w': _L0_attn_in['o_w'], 'L0_attn_o_b': _L0_attn_in['o_b'], 'L0_attn_pos': _L0_attn_in['pos'], 'L0_attn_zero': _L0_attn_in['zero'], 'L0_attn_neg': _L0_attn_in['neg'], 'L0_xattn_Wq': _L0_xattn_in['Wq'], 'L0_xattn_bq': _L0_xattn_in['bq'], 'L0_xattn_Wk': _L0_xattn_in['Wk'], 'L0_xattn_bk': _L0_xattn_in['bk'], 'L0_xattn_Wv': _L0_xattn_in['Wv'], 'L0_xattn_bv': _L0_xattn_in['bv'], 'L0_xattn_Wo': _L0_xattn_in['Wo'], 'L0_xattn_bo': _L0_xattn_in['bo'], 'L0_ffn_W1': _L0_ffn_in['W1'], 'L0_ffn_W2': _L0_ffn_in['W2'], 'L0_ffn_Wr': _L0_ffn_in['Wr']}

def reference(x, ctx_1024, L0_attn_key, L0_attn_value, L0_attn_u_w, L0_attn_u_b, L0_attn_v_w, L0_attn_v_b, L0_attn_o_w, L0_attn_o_b, L0_attn_pos, L0_attn_zero, L0_attn_neg, L0_xattn_Wq, L0_xattn_bq, L0_xattn_Wk, L0_xattn_bk, L0_xattn_Wv, L0_xattn_bv, L0_xattn_Wo, L0_xattn_bo, L0_ffn_W1, L0_ffn_W2, L0_ffn_Wr):
    import jax
    import jax.numpy as jnp

    def _L0_attn_ref(query, key, value, u_w, u_b, v_w, v_b, o_w, o_b, pos, zero, neg):
        import jax, jax.numpy as jnp
        import numpy as np
        L, B, E, H = (1024, 4, 512, 8)
        D1 = 2 * E
        EPS = 1e-08

        def _toeplitz_mix(v, pos, zero, neg):
            b, h, n, d = v.shape
            m = 2 * n
            a = jnp.concatenate([zero, pos[:, :n - 1], jnp.zeros((h, 1), v.dtype), neg[:, :n - 1][:, ::-1]], axis=-1)
            af = jnp.fft.rfft(a, n=m, axis=-1)
            vf = jnp.fft.rfft(v, n=m, axis=-2)
            y = jnp.fft.irfft(af[None, :, :, None] * vf, n=m, axis=-2)
            return y[:, :, :n, :]
        n, b, e = query.shape
        rms = jnp.linalg.norm(query, axis=-1, keepdims=True) * e ** (-0.5)
        x = query / (rms + EPS)
        u = jax.nn.silu(jnp.einsum('nbe,fe->nbf', x, u_w) + u_b)
        v = jax.nn.silu(jnp.einsum('nbe,fe->nbf', x, v_w) + v_b)
        hd = v.shape[-1] // H
        vh = v.reshape(n, b, H, hd).transpose(1, 2, 0, 3)
        y = _toeplitz_mix(vh, pos, zero, neg)
        y = y.transpose(2, 0, 1, 3).reshape(n, b, H * hd)
        out = u * y
        return jnp.einsum('nbf,ef->nbe', out, o_w) + o_b + query

    def _L0_xattn_ref(queries, keys, values, Wq, bq, Wk, bk, Wv, bv, Wo, bo):
        import jax, jax.numpy as jnp
        import numpy as np
        import math
        D_MODEL = 512
        N_HEADS = 16
        N, L, _ = queries.shape
        S = keys.shape[1]
        H = N_HEADS
        q = (queries @ Wq.T + bq).reshape(N, L, H, -1)
        k = (keys @ Wk.T + bk).reshape(N, S, H, -1)
        v = (values @ Wv.T + bv).reshape(N, S, H, -1)
        D = k.shape[-1]
        sm = jnp.einsum('nlhd,nshd->nlhs', q, k) / math.sqrt(D)
        causal_mask = jnp.triu(jnp.ones((L, S), dtype=bool), k=1)
        sm = jnp.where(causal_mask[None, :, None, :], -jnp.inf, sm)
        sm = jax.nn.softmax(sm, axis=-1)
        attn = jnp.einsum('nlhs,nshd->nlhd', sm, v)
        new_values = attn.reshape(N, L, H * D)
        return new_values @ Wo.T + bo

    def _L0_ffn_ref(x, W1, W2, Wr):
        import jax, jax.numpy as jnp
        import numpy as np
        B, T, D = (2, 1024, 512)
        E, DFF, TOPK = (8, 2048, 2)
        TEMPERATURE = 1.0
        logits = jnp.einsum('btd,ed->bte', x, Wr)
        probs = jax.nn.softmax(logits / TEMPERATURE, axis=-1)
        topk_vals, topk_idx = jax.lax.top_k(probs, TOPK)
        router_weights = topk_vals / topk_vals.sum(-1, keepdims=True)
        one_hot = jax.nn.one_hot(topk_idx, E, dtype=x.dtype)
        gate = jnp.einsum('btk,btke->bte', router_weights, one_hot)
        h = jax.nn.silu(jnp.einsum('btd,efd->btef', x, W1))
        y = jnp.einsum('btef,edf->bted', h, W2)
        out = jnp.einsum('bte,bted->btd', gate, y)
        return out
    x = _layernorm(x + _L0_attn_ref(x, L0_attn_key, L0_attn_value, L0_attn_u_w, L0_attn_u_b, L0_attn_v_w, L0_attn_v_b, L0_attn_o_w, L0_attn_o_b, L0_attn_pos, L0_attn_zero, L0_attn_neg), axis=-1)
    x = _layernorm(x + _L0_xattn_ref(x, ctx_1024, ctx_1024, L0_xattn_Wq, L0_xattn_bq, L0_xattn_Wk, L0_xattn_bk, L0_xattn_Wv, L0_xattn_bv, L0_xattn_Wo, L0_xattn_bo), axis=-1)
    x = _layernorm(x + _L0_ffn_ref(x, L0_ffn_W1, L0_ffn_W2, L0_ffn_Wr), axis=-1)
    return x

_drawn_inputs = setup_inputs


def setup_inputs(seed=0):
    import zlib

    import numpy as np

    out = dict(_drawn_inputs(seed))
    spreads = {}
    factors = {'L0_attn_u_w': 8.0,
     'L0_attn_u_b': 8.0,
     'L0_attn_v_w': 8.0,
     'L0_attn_v_b': 8.0,
     'L0_attn_o_w': 8.0,
     'L0_attn_o_b': 14.914,
     'L0_attn_pos': 8.0,
     'L0_attn_zero': 8.0,
     'L0_attn_neg': 8.0,
     'L0_xattn_bq': 3.509,
     'L0_xattn_bk': 64.0}
    for name, (base, spread) in spreads.items():
        noise = np.random.default_rng([zlib.crc32(name.encode()), seed]).standard_normal(out[name].shape)
        drawn = base * np.exp(spread * noise) if base else spread * noise
        out[name] = jnp.asarray(drawn.astype(out[name].dtype))
    for name, factor in factors.items():
        out[name] = (out[name] * factor).astype(out[name].dtype)
    return out
```

```python
import numpy as np

import concourse.bass as bass
from concourse import mybir

F32 = mybir.dt.float32
F32R = mybir.dt.float32r
I32 = mybir.dt.int32
ALU = mybir.AluOpType
ACT = mybir.ActivationFunctionType
AX = mybir.AxisListType.X

P = 128
N, L, D = 8, 100, 512
T = N * L
HT = T // 2
KD = D // P
TILES = -(-T // P)
FULL = T // P
LAST = T - FULL * P
F1 = 2 * D
MH = F1 // P
BS = P // N
AH, AD = 16, 32
G4 = AH // 4
E, DFF = 8, 2048
CAP = 256
CT = CAP // P
PASSES = -(-T // CAP)
BLOCKS = PASSES * E
RING = 4
EPS = 1e-5
MASKED = -1e30

V0, U0, U1, V1, O0, O1, WK, CTX0, CTX1, WQ, WV, WO = range(12)
FIRST = 12
ORDER = [(1, 0), (1, 1), (2, 0), (1, 2), (2, 1), (1, 3), (2, 2), (2, 3)]
PER = len(ORDER)
W1_PIECE = [ORDER.index((1, q)) for q in range(4)]
W2_PIECE = [ORDER.index((2, q)) for q in range(4)]
EXTRA = 2


def rows(t):
    return min(P, T - t * P)


def decoder_layer(nc, x_tok, x_feat, pieces, ffn_pieces, u_b, v_b, o_b, mix_taps, bq, bk, bv_bo,
                  router_w, out):
    routed = nc.dram_tensor("routed", (BLOCKS * CAP, D), F32, kind="Internal").ap()
    expert_out = nc.dram_tensor("expert_out", (BLOCKS * CAP, D), F32, kind="Internal").ap()

    top = [-(-nc.sbuf_base // 64) * 64]

    def sb(name, shape, dt=F32, offset=None):
        if offset is None:
            offset = top[0]
            top[0] += -(-int(np.prod(shape[1:])) * 4 // 32) * 32
        return nc.alloc_sbuf_tensor_at(name, list(shape), dt, offset=offset)

    FEAT = KD * T * 4
    raw = [sb(f"raw{i}", [P, 2048]) for i in range(RING)]
    whi = [sb(f"whi{i}", [P, 2048], F32R) for i in range(RING)]
    wlo = [sb(f"wlo{i}", [P, 2048], F32R) for i in range(RING)]
    region_a = top[0]
    xf_hi = sb("xf_hi", [P, KD, T], F32R)
    xf_lo = sb("xf_lo", [P, KD, T], F32R)
    region_b = top[0]
    gated0_hi = sb("gated0_hi", [P, KD, T], F32R)
    gated0_lo = sb("gated0_lo", [P, KD, T], F32R)
    region_c = top[0]
    u_feat = sb("u_feat", [P, KD, T])
    v_tok = sb("v_tok", [P, TILES, 512])
    x = sb("x", [P, TILES, D])
    gated1_hi = sb("gated1_hi", [P, KD, T], F32R, region_a)
    gated1_lo = sb("gated1_lo", [P, KD, T], F32R, region_a + FEAT)
    k_feat = sb("k_feat", [P, KD, T], F32, region_a)
    q_feat = sb("q_feat", [P, KD, T], F32, region_a + FEAT)
    x2_feat = sb("x2_feat", [P, KD, T], F32, region_a)
    squares = sb("squares", [P, KD, T], F32, region_b)
    probs = sb("probs", [L, 2, AH * L], F32, region_b)
    probs_t = sb("probs_t", [L, 2, 2, AH * L // 2], F32, region_b + 2 * AH * L * 4)
    x_f = sb("x_f", [P, KD, T], F32, region_c)
    x1_hi = sb("x1_hi", [P, KD, T], F32R, region_c)
    x1_lo = sb("x1_lo", [P, KD, T], F32R, region_c + FEAT)
    att_hi = sb("att_hi", [P, KD, T], F32R, region_c)
    att_lo = sb("att_lo", [P, KD, T], F32R, region_c + FEAT)
    moe_top = [region_a]

    def sb_moe(name, shape, dt=F32):
        o = moe_top[0]
        moe_top[0] += int(np.prod(shape[1:])) * 4
        assert moe_top[0] <= region_c
        return sb(name, shape, dt, o)

    xg = sb_moe("xg", [P, CT, D])
    xg_hi = sb_moe("xg_hi", [P, KD, CAP], F32R)
    xg_lo = sb_moe("xg_lo", [P, KD, CAP], F32R)
    hidden = sb_moe("hidden", [P, 2, 4, CAP])
    h_hi = sb_moe("h_hi", [P, 2, 4, CAP], F32R)
    h_lo = sb_moe("h_lo", [P, 2, 4, CAP], F32R)
    y_sb = sb_moe("y_sb", [P, CT, D])
    picked = sb("picked", [P, TILES, 2, D], F32, region_a)

    v_bias_at = top[0]
    v_bias = sb("v_bias", [P, F1])
    att_bias = sb("att_bias", [P, 2, D], F32, v_bias_at)
    mix_at = top[0]
    mix = sb("mix", [P, MH, P])
    v_att = sb("v_att", [L, 2, D], F32, mix_at)
    o_bias = sb("o_bias", [P, D])
    o_att = sb("o_att", [L, D], F32)
    ident = sb("ident", [P, P])
    ones = sb("ones", [P, P])
    before = sb("before", [P, P])
    scale_row = sb("scale_row", [P, T])
    scale_col = sb("scale_col", [P, TILES])
    causal = sb("causal", [L, L])
    zeros = sb("zeros", [P, D])
    taps = sb("taps", [P, MH * N])
    same_b = sb("same_b", [P, BS])
    ub_col = sb("ub_col", [P, MH])
    bq_col = sb("bq_col", [P, KD])
    bk_col = sb("bk_col", [P, KD])
    eps_col = sb("eps_col", [P, 1])
    wr = sb("wr", [P, KD, E])
    lower = sb("lower", [P, E, E])
    first_row = sb("first_row", [P, E])
    valid = sb("valid", [P, TILES, 1])
    bn = sb("bn", [P, 2, 6])
    mv = sb("mv", [P, 2, 2])
    std = sb("std", [P, 2])
    rstd = sb("rstd", [P, 2])
    row_max = sb("row_max", [L, 2, AH])
    row_sum = sb("row_sum", [L, 2, AH])
    n_blocks = sb("n_blocks", [P, 1], I32)
    row1 = sb("row1", [P, TILES], I32)
    row2 = sb("row2", [P, TILES], I32)
    gate1 = sb("gate1", [P, TILES])
    gate2 = sb("gate2", [P, TILES])
    assert top[0] <= nc.sbuf_usable_end, top[0]
    router_top = [region_c]

    def sb_router(name, shape):
        o = router_top[0]
        router_top[0] += -(-int(np.prod(shape[1:])) * 4 // 32) * 32
        assert router_top[0] <= region_c + 2 * FEAT
        return sb(name, shape, F32, o)

    S3 = [P, TILES, E]
    logits = sb_router("logits", S3)
    lg_exp = sb_router("lg_exp", S3)
    prob = sb_router("prob", S3)
    t_a = sb_router("t_a", S3)
    rank = sb_router("rank", S3)
    pick1 = sb_router("pick1", S3)
    pick2 = sb_router("pick2", S3)
    sel = sb_router("sel", [P, TILES + 1, E])
    place = sb_router("place", S3)
    over = sb_router("over", S3)
    over2 = sb_router("over2", S3)
    gt = sb_router("gt", [P, TILES, E * E])
    eq = sb_router("eq", [P, TILES, E * E])
    r_col = sb_router("r_col", [P, TILES])
    r_col2 = sb_router("r_col2", [P, TILES])
    m_col = sb_router("m_col", [P, 4])

    bank = nc.alloc_psum_tensor("bank", [P, 8, 512], F32)

    def sem(name):
        return nc.alloc_semaphore(name)

    x_in, small_in, bias2_in = sem("x_in"), sem("small_in"), sem("bias2_in")
    xt_in = [sem(f"xt_in{hf}") for hf in range(2)]
    consts = sem("consts")
    w_in = [sem(f"w_in{i}") for i in range(RING)]
    w_hi, w_lo = sem("w_hi"), sem("w_lo")
    sq_done, ssq_mm, rms_done = sem("sq_done"), sem("ssq_mm"), sem("rms_done")
    xf_hi_done, xf_lo_done, mix_done = sem("xf_hi_done"), sem("xf_lo_done"), sem("mix_done")
    u_mm, u_scaled, u_act = sem("u_mm"), sem("u_scaled"), sem("u_act")
    v_mm, v_biased, v_act = sem("v_mm"), sem("v_biased"), sem("v_act")
    y_mm, y_gated, y_hi, y_lo = sem("y_mm"), sem("y_gated"), sem("y_hi"), sem("y_lo")
    res1 = sem("res1")
    o_mm, r1_done, var1, std1, x1_done = sem("o_mm"), sem("r1_done"), sem("var1"), sem("std1"), sem("x1_done")
    x1t_mm, x1t_hi, x1t_lo = sem("x1t_mm"), sem("x1t_hi"), sem("x1t_lo")
    kq_mm, kq_done = sem("kq_mm"), sem("kq_done")
    res2 = sem("res2")
    va_mm, va_done = sem("va_mm"), sem("va_done")
    s_mm, s_read, s_max, s_sub, s_exp, s_sum = (sem(s) for s in
                                                ("s_mm", "s_read", "s_max", "s_sub", "s_exp", "s_sum"))
    pt_mm, pt_done, pv_mm, pv_done = sem("pt_mm"), sem("pt_done"), sem("pv_mm"), sem("pv_done")
    at_mm, at_hi, at_lo = sem("at_mm"), sem("at_hi"), sem("at_lo")
    o2_mm, r2_done, var2, std2, x2_done = sem("o2_mm"), sem("r2_done"), sem("var2"), sem("std2"), sem("x2_done")
    x2t_mm, x2t_done, lg_mm = sem("x2t_mm"), sem("x2t_done"), sem("lg_mm")
    lg_shift, lg_exped, sel_done, rank_mm = sem("lg_shift"), sem("lg_exped"), sem("sel_done"), sem("rank_mm")
    rows_ready, blocks_ready = sem("rows_ready"), sem("blocks_ready")
    zero_set, zeroed, scattered = sem("zero_set"), sem("zeroed"), sem("scattered")
    block_begun = sem("block_begun")
    defined, all_out = sem("defined"), sem("all_out")
    xg_in = sem("xg_in")
    xgt_mm, xgt_hi, xgt_lo = sem("xgt_mm"), sem("xgt_hi"), sem("xgt_lo")
    g1_mm, h_act, h_split_hi, h_split = sem("g1_mm"), sem("h_act"), sem("h_split_hi"), sem("h_split")
    g2_mm, y_read, y_out = sem("g2_mm"), sem("y_read"), sem("y_out")
    pick_in = [sem(f"pick_in{t}") for t in range(TILES)]
    var3, std3, out_ready, out_done = sem("var3"), sem("std3"), sem("out_ready"), sem("out_done")
    dve_step = sem("dve_step")

    def released(i):
        if i < FIRST:
            return {U0: (u_mm, 8), V0: (v_mm, TILES), U1: (u_mm, 16), V1: (v_mm, 2 * TILES),
                    O0: (o_mm, TILES), O1: (o_mm, TILES), WK: (kq_mm, 8), CTX0: (va_mm, N // 2),
                    CTX1: (va_mm, N), WQ: (kq_mm, 16), WV: (va_mm, N), WO: (o2_mm, TILES)}[i]
        return expert_piece_released(0, i - FIRST)

    def expert_piece_released(g, j):
        back = 1 if isinstance(j, int) and j < 0 else 0
        which, q = ORDER[j % PER]
        if which == 1:
            return g1_mm, (g - back) * 8 + 2 * q + 2
        return g2_mm, (g - back) * 4 + q + 1

    bc = lambda ap, shape: ap.broadcast_to(list(shape))

    with nc.Block() as block:

        @block.sync
        def _(sp):
            def load_piece(i):
                if i >= RING:
                    sp.wait_ge(w_lo, i - RING + 1)
                src = pieces[i] if i < FIRST else ffn_pieces[i - FIRST]
                sp.dma_start(raw[i % RING][:], src).then_inc(w_in[i % RING], 16)

            def load_x(hf):
                sp.dma_start(x_f[:, :, hf * HT:(hf + 1) * HT], x_feat[:, :, hf * HT:(hf + 1) * HT])\
                  .then_inc(xt_in[hf], 16)

            load_x(0)
            load_piece(V0)
            load_x(1)
            sp.dma_start(v_bias[:], v_b.partition_broadcast(P)).then_inc(small_in, 16)
            sp.dma_start(ub_col[:], u_b).then_inc(small_in, 16)
            sp.dma_start(taps[:], mix_taps).then_inc(small_in, 16)
            sp.dma_start(bq_col[:], bq).then_inc(small_in, 16)
            sp.dma_start(bk_col[:], bk).then_inc(small_in, 16)
            sp.dma_start(wr[:], router_w).then_inc(small_in, 16)
            load_piece(U0)
            load_piece(U1)
            load_piece(V1)
            sp.dma_start(x[:, 0:FULL, :], x_tok[0:FULL * P].rearrange("(t p) d -> p t d", p=P)).then_inc(x_in, 16)
            sp.dma_start(x[0:LAST, FULL, :], x_tok[FULL * P:T]).then_inc(x_in, 16)
            sp.dma_start(o_bias[:], o_b.partition_broadcast(P)).then_inc(x_in, 16)
            load_piece(O0)
            sp.wait_ge(zero_set, 1)
            for g in range(E):
                sp.dma_start(routed[g * CAP:(g + 1) * CAP].rearrange("(n p) d -> p n d", p=P),
                             bc(zeros[:].unsqueeze(1), [P, CT, D])).then_inc(zeroed, 16)
            load_piece(O1)
            load_piece(WK)
            load_piece(CTX0)
            sp.wait_ge(v_biased, 2 * TILES)
            sp.dma_start(att_bias[:], bv_bo.partition_broadcast(P)).then_inc(bias2_in, 16)
            for i in range(CTX1, FIRST + 2):
                load_piece(i)

            def load_expert_pieces(g):
                for j in range(EXTRA, PER + EXTRA):
                    i = FIRST + j
                    sp.wait_ge(w_lo, g * PER + (i - RING + 1))
                    if j == EXTRA:
                        sp.sem_inc(block_begun, 1)
                    src = ffn_pieces[bass.ds((g & (E - 1)) * PER + j, 1)].rearrange("a p n -> (a p) n")
                    sp.dma_start(raw[i % RING][:], src).then_inc(w_in[i % RING], 16)

            for j in range(EXTRA, RING):
                i = FIRST + j
                sp.wait_ge(w_lo, i - RING + 1)
                sp.dma_start(raw[i % RING][:], ffn_pieces[j]).then_inc(w_in[i % RING], 16)
            sp.wait_ge(blocks_ready, 1)
            blocks = sp.value_load(n_blocks[0:1, 0:1], min_val=E, max_val=BLOCKS)
            sp.wait_ge(zeroed, 16 * E)
            with sp.Fori(E - 1, blocks) as g:
                sp.dma_start(routed[bass.ds(g * CAP, CAP)].rearrange("(n p) d -> p n d", p=P),
                             bc(zeros[:].unsqueeze(1), [P, CT, D])).then_inc(zeroed, 16)
            for j in range(RING, PER + EXTRA):
                i = FIRST + j
                sp.wait_ge(w_lo, i - RING + 1)
                sp.dma_start(raw[i % RING][:], ffn_pieces[j]).then_inc(w_in[i % RING], 16)
            with sp.Fori(1, blocks) as g:
                load_expert_pieces(g)
            for t in range(TILES):
                sp.wait_ge(out_ready, t + 1)
                sp.dma_start(out[t * P:t * P + rows(t)], x[0:rows(t), t, :]).then_inc(out_done, 16)
            sp.wait_ge(out_done, 16 * TILES)

        @block.gpsimd
        def _(pool):
            pool.memset(ident[:], 0.0).then_inc(consts, 1)
            pool.memset(ones[:], 1.0).then_inc(consts, 1)
            pool.memset(before[:], 1.0).then_inc(consts, 1)
            pool.memset(causal[:], 0.0).then_inc(consts, 1)
            pool.memset(lower[:], 1.0).then_inc(consts, 1)
            pool.memset(valid[:], 1.0).then_inc(consts, 1)
            pool.memset(eps_col[:], EPS).then_inc(consts, 1)
            pool.iota(first_row[:], [[CAP, E]], base=0, channel_multiplier=0,
                      allow_small_or_imprecise_dtypes=True).then_inc(consts, 1)
            pool.wait_ge(consts, 8)
            pool.affine_select(out=ident[:], in_=ident[:], compare_op=ALU.not_equal, fill=1.0, base=0,
                               pattern=[[-1, P]], channel_multiplier=1).then_inc(consts, 1)
            pool.affine_select(out=before[:], in_=before[:], compare_op=ALU.is_gt, fill=0.0, base=0,
                               pattern=[[1, P]], channel_multiplier=-1).then_inc(consts, 1)
            pool.affine_select(out=causal[:], in_=causal[:], compare_op=ALU.is_ge, fill=MASKED, base=0,
                               pattern=[[-1, L]], channel_multiplier=1).then_inc(consts, 1)
            pool.affine_select(out=lower[:], in_=lower[:], compare_op=ALU.is_gt, fill=0.0, base=0,
                               pattern=[[1, E], [-1, E]], channel_multiplier=0).then_inc(consts, 1)
            pool.affine_select(out=valid[:, :, 0], in_=valid[:, :, 0], compare_op=ALU.is_ge, fill=0.0,
                               base=T - 1, pattern=[[-P, TILES]], channel_multiplier=-1).then_inc(consts, 1)
            pool.memset(zeros[:], 0.0).then_inc(zero_set, 1)

            for hf in range(2):
                a = x_f[:, :, hf * HT:(hf + 1) * HT]
                pool.wait_ge(xt_in[hf], 16)
                pool.tensor_tensor(squares[:, :, hf * HT:(hf + 1) * HT], a, a, ALU.mult).then_inc(sq_done, 1)
            pool.wait_ge(x_in, 48)
            for r, ts in ((P, slice(0, FULL)), (LAST, slice(FULL, TILES))):
                a = x[0:r, ts, :]
                pool.tensor_tensor(a, a, a, ALU.add).then_inc(res1, 1)
            pool.wait_ge(res1, 2)
            for r, ts in ((P, slice(0, FULL)), (LAST, slice(FULL, TILES))):
                a = x[0:r, ts, :]
                pool.tensor_tensor(a, a, bc(o_bias[0:r].unsqueeze(1), a.shape), ALU.add).then_inc(res1, 1)
            pool.wait_ge(bias2_in, 16)
            pool.wait_ge(x1t_mm, TILES)
            for r, ts in ((P, slice(0, FULL)), (LAST, slice(FULL, TILES))):
                a = x[0:r, ts, :]
                pool.tensor_tensor(a, a, bc(att_bias[0:r, 1:2, :], a.shape), ALU.add).then_inc(res2, 1)
            for n in range(N):
                pool.wait_ge(s_max, n + 1)
                s = probs[:, n % 2, :].rearrange("l (h s) -> l h s", s=L)
                pool.tensor_tensor(s, s, bc(row_max[:, n % 2, :].unsqueeze(2), [L, AH, L]), ALU.subtract)\
                    .then_inc(s_sub, 1)

            pool.wait_ge(blocks_ready, 1)
            blocks = pool.value_load(n_blocks[0:1, 0:1], min_val=E, max_val=BLOCKS)
            pool.wait_ge(rows_ready, 1)
            pool.wait_ge(zeroed, blocks * 16 + 16)
            pool.sem_inc(defined, 1)
            pool.wait_ge(defined, 1)
            for t in range(TILES):
                for to in (row1, row2):
                    pool.indirect_dma_start(
                        out=routed, out_offset=bass.IndirectOffsetOnAxis(ap=to[0:rows(t), t:t + 1], axis=0),
                        in_=x[0:rows(t), t, :], in_offset=None).then_inc(scattered, 16)
            pool.wait_ge(scattered, 32 * TILES)
            pool.dma_start(xg[:], routed[0:CAP].rearrange("(s p) d -> p s d", p=P)).then_inc(xg_in, 16)
            with pool.Fori(1, blocks) as g:
                pool.wait_ge(xgt_mm, g * 2)
                pool.dma_start(xg[:], routed[bass.ds(g * CAP, CAP)].rearrange("(s p) d -> p s d", p=P))\
                    .then_inc(xg_in, 16)
            pool.wait_ge(y_out, blocks * 16)
            pool.sem_inc(all_out, 1)
            pool.wait_ge(all_out, 1)
            def pick(written):
                for t in range(TILES):
                    for c, frm in enumerate((row1, row2)):
                        pool.indirect_dma_start(
                            out=picked[0:rows(t), t, c, :], out_offset=None, in_=written,
                            in_offset=bass.IndirectOffsetOnAxis(ap=frm[0:rows(t), t:t + 1], axis=0))\
                            .then_inc(pick_in[t], 16)

            with pool.If(blocks < E + 1):
                pick(expert_out[0:E * CAP])
            with pool.Else():
                pick(expert_out)

        @block.scalar
        def _(act):
            def split_hi(i):
                act.wait_ge(w_in[i % RING], 16 * (i // RING + 1))
                if i >= RING:
                    act.wait_ge(*released(i - RING))
                act.activation(whi[i % RING][:], raw[i % RING][:], ACT.Copy).then_inc(w_hi, 1)

            def x_hi(hf):
                cols = slice(hf * HT, (hf + 1) * HT)
                act.wait_ge(xt_in[hf], 16)
                act.activation(xf_hi[:, :, cols], x_f[:, :, cols], ACT.Copy).then_inc(xf_hi_done, 1)

            def v_silu(g, t):
                act.wait_ge(v_biased, TILES * g + t + 1)
                act.activation(v_tok[0:rows(t), t, :], v_tok[0:rows(t), t, :], ACT.Silu).then_inc(v_act, 1)

            def u_silu(g, n):
                j, hf = n // 2, n % 2
                a = u_feat[:, j, hf * HT:(hf + 1) * HT]
                act.wait_ge(u_scaled, 8 * g + n + 1)
                act.activation(a, a, ACT.Silu, bias=ub_col[:, 4 * g + j:4 * g + j + 1]).then_inc(u_act, 1)

            def gated_hi(g, j):
                act.wait_ge(y_gated, 4 * g + j + 1)
                act.activation((gated1_hi if g else gated0_hi)[:, j, :], u_feat[:, j, :], ACT.Copy)\
                   .then_inc(y_hi, 1)

            x_hi(0)
            split_hi(V0)
            x_hi(1)
            act.wait_ge(ssq_mm, 1)
            act.activation(scale_col[:, 0:FULL], bank[:, 2, 0:FULL], ACT.Sqrt, scale=1.0 / D)
            act.activation(scale_col[0:LAST, FULL:], bank[0:LAST, 2, FULL:TILES], ACT.Sqrt, scale=1.0 / D)\
               .then_inc(rms_done, 1)
            for hf in range(2):
                act.wait_ge(ssq_mm, hf + 2)
                act.activation(scale_row[:, hf * HT:(hf + 1) * HT], bank[:, hf, 0:HT], ACT.Sqrt, scale=1.0 / D)\
                   .then_inc(rms_done, 1)
            split_hi(U0)
            for t in range(3):
                v_silu(0, t)
            split_hi(U1)
            for t in range(3, TILES):
                v_silu(0, t)
            split_hi(V1)
            act.wait_ge(small_in, 96)
            for n in range(8):
                u_silu(0, n)
            split_hi(O0)
            split_hi(O1)
            gated_hi(0, 0)
            for j in range(4):
                if j < 3:
                    gated_hi(0, j + 1)
                u_silu(1, 2 * j)
                u_silu(1, 2 * j + 1)
            split_hi(WK)
            for t in range(TILES):
                v_silu(1, t)
            split_hi(CTX0)
            for j in range(4):
                gated_hi(1, j)

            act.wait_ge(consts, 13)
            for t in range(TILES):
                r = rows(t)
                act.wait_ge(var1, t + 1)
                act.activation(std[0:r, t % 2:t % 2 + 1], mv[0:r, t % 2, 1:2], ACT.Sqrt,
                               bias=eps_col[0:r, :]).then_inc(std1, 1)
                if t == TILES - 2:
                    split_hi(CTX1)
                    split_hi(WQ)

            def kq(i):
                c, n = divmod(i, 8)
                j, hf = (n % 4, n // 4)
                act.wait_ge(kq_mm, i + 1)
                to, frm = k_feat[:, j, hf * HT:(hf + 1) * HT], bank[:, 6 + i % 2, 0:HT]
                if c:
                    to = q_feat[:, j, :].rearrange("p (n l) -> p n l", n=N)[:, :, hf * L // 2:(hf + 1) * L // 2]
                    frm = frm.rearrange("p (l n) -> p n l", n=N)
                act.activation(to, frm, ACT.Identity, bias=(bq_col if c else bk_col)[:, j:j + 1])\
                   .then_inc(kq_done, 1)

            for i in range(8):
                kq(i)
            for t in range(TILES):
                r = rows(t)
                act.wait_ge(x1t_mm, t + 1)
                act.activation(x1_hi[:, :, t * P:t * P + r],
                               bank[:, 4 + t % 2, :].rearrange("p (k c) -> p k c", k=KD)[:, :, 0:r],
                               ACT.Copy).then_inc(x1t_hi, 1)
            split_hi(WV)
            for i in range(8, 16):
                kq(i)

            def exp_of(n):
                act.wait_ge(s_sub, n + 1)
                act.activation(probs[:, n % 2, :], probs[:, n % 2, :], ACT.Exp, scale=float(AD) ** -0.5)\
                   .then_inc(s_exp, 1)

            def turned(n, r):
                act.wait_ge(pt_mm, 2 * n + r + 1)
                if n >= 2:
                    act.wait_ge(pv_mm, n - 1)
                act.activation(probs_t[:, n % 2, r, :].rearrange("s (j c) -> s j c", j=2),
                               bank[0:L, 4:6, 0:G4 * L], ACT.Copy).then_inc(pt_done, 1)

            def attended_hi(n):
                act.wait_ge(at_mm, n + 1)
                act.activation(att_hi[:].rearrange("p k (l n) -> p k l n", n=N)[:, :, :, n],
                               bank[:, 7, 0:KD * L].rearrange("p (k c) -> p k c", k=KD), ACT.Copy)\
                   .then_inc(at_hi, 1)

            exp_of(0)
            for n in range(N):
                turned(n, 0)
                if n:
                    attended_hi(n - 1)
                if n + 1 < N:
                    exp_of(n + 1)
                turned(n, 1)
                if n == N // 2:
                    split_hi(WO)
            attended_hi(N - 1)
            split_hi(FIRST)
            split_hi(FIRST + 1)

            def x2_out_of_psum(t):
                r = rows(t)
                act.wait_ge(x2t_mm, t + 1)
                act.activation(x2_feat[:, :, t * P:t * P + r],
                               bank[:, 4 + t % 2, :].rearrange("p (k c) -> p k c", k=KD)[:, :, 0:r],
                               ACT.Copy).then_inc(x2t_done, 1)

            for t in range(TILES):
                r = rows(t)
                act.wait_ge(var2, t + 1)
                act.activation(std[0:r, t % 2:t % 2 + 1], mv[0:r, t % 2, 1:2], ACT.Sqrt,
                               bias=eps_col[0:r, :]).then_inc(std2, 1)
                if t:
                    x2_out_of_psum(t - 1)
            x2_out_of_psum(TILES - 1)
            act.wait_ge(lg_shift, 1)
            act.activation(lg_exp[:], t_a[:], ACT.Exp).then_inc(lg_exped, 1)

            def expert_hi(g, j):
                i = FIRST + j
                act.wait_ge(w_in[i % RING], (g * 2 + (i // RING + 1)) * 16)
                if j >= RING or not isinstance(g, int):
                    act.wait_ge(*expert_piece_released(g, j - RING))
                else:
                    act.wait_ge(*released(i - RING))
                act.activation(whi[i % RING][:], raw[i % RING][:], ACT.Copy).then_inc(w_hi, 1)

            def expert(g):
                first = isinstance(g, int)
                for b in range(2):
                    act.wait_ge(xgt_mm, g * 2 + b + 1)
                    act.activation(xg_hi[:, 2 * b:2 * b + 2, :],
                                   bank[:, 6 + b, :].rearrange("p (k c) -> p k c", k=2), ACT.Copy)\
                       .then_inc(xgt_hi, 1)
                expert_hi(g, 2)
                if not first:
                    results(g)
                expert_hi(g, 3)
                for q, ahead in ((0, (4,)), (1, (5, 6)), (2, (7, 8)), (3, (9,))):
                    for b in range(2):
                        act.wait_ge(g1_mm, g * 8 + (2 * q + b + 1))
                        if not first or q >= 2:
                            act.wait_ge(h_split, g * 4 + (q - 1))
                        act.activation(hidden[:, q % 2, 2 * b:2 * b + 2, :],
                                       bank[:, 2 * (q % 2) + b, :].rearrange("p (f c) -> p f c", f=2),
                                       ACT.Silu).then_inc(h_act, 1)
                    for j in ahead:
                        expert_hi(g, j)

            def results(g):
                act.wait_ge(g2_mm, g * 4)
                act.activation(y_sb[:], bank[:, 4:6, :], ACT.Copy).then_inc(y_read, 1)
                act.wait_ge(y_read, g)
                act.dma_start(expert_out[bass.ds((g - 1) * CAP, CAP)].rearrange("(s p) d -> p s d", p=P),
                              y_sb[:]).then_inc(y_out, 16)

            expert(0)
            blocks = act.value_load(n_blocks[0:1, 0:1], min_val=E, max_val=BLOCKS)
            with act.Fori(1, blocks) as g:
                expert(g)
                act.wait_ge(y_out, g * 16)
            results(blocks)
            for t in range(TILES):
                r = rows(t)
                act.wait_ge(var3, t + 1)
                act.activation(std[0:r, t % 2:t % 2 + 1], mv[0:r, t % 2, 1:2], ACT.Sqrt,
                               bias=eps_col[0:r, :]).then_inc(std3, 1)

        @block.vector
        def _(dve):
            steps = [0]

            def link(ins):
                steps[0] += 1
                ins.then_inc(dve_step, 1)
                dve.wait_ge(dve_step, steps[0])

            def f(ap):
                return ap.bitcast(F32)

            def split_lo(i):
                dve.wait_ge(w_hi, i + 1)
                dve.tensor_tensor(wlo[i % RING][:], raw[i % RING][:], f(whi[i % RING][:]), ALU.subtract)\
                   .then_inc(w_lo, 1)

            def x_lo(hf):
                cols = slice(hf * HT, (hf + 1) * HT)
                dve.wait_ge(xf_hi_done, hf + 1)
                dve.tensor_tensor(xf_lo[:, :, cols], x_f[:, :, cols], f(xf_hi[:, :, cols]), ALU.subtract)\
                   .then_inc(xf_lo_done, 1)

            def v_scale(g, t):
                r = rows(t)
                dve.wait_ge(v_mm, TILES * g + t + 1)
                if g and t == 0:
                    dve.wait_ge(y_mm, 4)
                dve.scalar_tensor_tensor(v_tok[0:r, t, :], bank[0:r, 4 + (TILES * g + t) % 2, :],
                                         scale_col[0:r, t:t + 1], v_bias[0:r, g * 512:(g + 1) * 512],
                                         ALU.mult, ALU.add).then_inc(v_biased, 1)

            def u_scale(g, n):
                j, hf = n // 2, n % 2
                cols = slice(hf * HT, (hf + 1) * HT)
                dve.wait_ge(u_mm, 8 * g + n + 1)
                if g:
                    dve.wait_ge(y_lo, j + 1)
                dve.tensor_tensor(u_feat[:, j, cols], bank[:, n % 4, 0:HT], scale_row[:, cols], ALU.mult)\
                   .then_inc(u_scaled, 1)

            def gate(g, j):
                hi, lo = (gated1_hi, gated1_lo) if g else (gated0_hi, gated0_lo)
                a = 6 if j % 2 == 0 else 4
                dve.wait_ge(y_mm, 4 * g + j + 1)
                dve.wait_ge(u_act, 8 * g + 2 * j + 2)
                for b_, c0 in ((a, 0), (a + 1, 512)):
                    u = u_feat[:, j, c0:min(c0 + 512, T)]
                    ins = dve.tensor_tensor(u, bank[:, b_, 0:u.shape[1]], u, ALU.mult)
                ins.then_inc(y_gated, 1)
                dve.wait_ge(y_hi, 4 * g + j + 1)
                dve.tensor_tensor(lo[:, j, :], u_feat[:, j, :], f(hi[:, j, :]), ALU.subtract).then_inc(y_lo, 1)

            x_lo(0)
            split_lo(V0)
            x_lo(1)
            dve.wait_ge(rms_done, 1)
            for r, ts in ((P, slice(0, FULL)), (LAST, slice(FULL, TILES))):
                link(dve.tensor_scalar(scale_col[0:r, ts], scale_col[0:r, ts], 1e-8, None, ALU.add))
                link(dve.reciprocal(scale_col[0:r, ts], scale_col[0:r, ts]))
            dve.wait_ge(small_in, 96)
            v_scale(0, 0)
            v_scale(0, 1)
            split_lo(U0)
            v_scale(0, 2)
            v_scale(0, 3)
            dve.wait_ge(rms_done, 3)
            link(dve.tensor_scalar(scale_row[:], scale_row[:], 1e-8, None, ALU.add))
            link(dve.reciprocal(scale_row[:], scale_row[:]))
            v_scale(0, 4)
            split_lo(U1)
            v_scale(0, 5)
            v_scale(0, 6)
            split_lo(V1)
            dve.wait_ge(consts, 13)
            link(dve.tensor_reduce(same_b[:], ident[:].rearrange("p (b i) -> p b i", i=N), AX, ALU.add))
            dve.tensor_tensor(mix[:].rearrange("p h (b i) -> p h b i", i=N),
                              bc(taps[:].rearrange("p (h i) -> p h i", i=N).unsqueeze(2), [P, MH, BS, N]),
                              bc(same_b[:].unsqueeze(1).unsqueeze(3), [P, MH, BS, N]), ALU.mult)\
                .then_inc(mix_done, 1)
            for n in range(8):
                u_scale(0, n)
            split_lo(O0)
            split_lo(O1)
            gate(0, 0)
            for j in range(4):
                if j < 3:
                    gate(0, j + 1)
                u_scale(1, 2 * j)
                u_scale(1, 2 * j + 1)
            split_lo(WK)
            for t in range(TILES):
                v_scale(1, t)
            split_lo(CTX0)
            for j in range(4):
                gate(1, j)

            def norm_stats(t, var):
                r, b = rows(t), t % 2
                link(dve.bn_stats(bn[0:r, b, :], x[0:r, t, :]))
                dve.bn_aggr(mv[0:r, b, :], bn[0:r, b, :]).then_inc(var, 1)

            def norm_apply(t, std_done, done):
                r, b = rows(t), t % 2
                dve.wait_ge(std_done, t + 1)
                link(dve.reciprocal(rstd[0:r, b:b + 1], std[0:r, b:b + 1]))
                dve.tensor_scalar(x[0:r, t, :], x[0:r, t, :], mv[0:r, b, 0:1], rstd[0:r, b:b + 1],
                                  ALU.subtract, ALU.mult).then_inc(done, 1)

            dve.wait_ge(res1, 4)
            for t in range(TILES):
                r = rows(t)
                dve.wait_ge(o_mm, t + 1)
                dve.tensor_tensor(x[0:r, t, :], bank[0:r, t % 4, :], x[0:r, t, :], ALU.add).then_inc(r1_done, 1)
                dve.wait_ge(r1_done, t + 1)
                norm_stats(t, var1)
                if t:
                    norm_apply(t - 1, std1, x1_done)
            norm_apply(TILES - 1, std1, x1_done)
            split_lo(CTX1)
            split_lo(WQ)
            for t in range(TILES):
                r = rows(t)
                dve.wait_ge(x1t_hi, t + 1)
                dve.tensor_tensor(x1_lo[:, :, t * P:t * P + r],
                                  bank[:, 4 + t % 2, :].rearrange("p (k c) -> p k c", k=KD)[:, :, 0:r],
                                  f(x1_hi[:, :, t * P:t * P + r]), ALU.subtract).then_inc(x1t_lo, 1)
            split_lo(WV)
            dve.wait_ge(bias2_in, 16)

            def values_biased(n):
                dve.wait_ge(va_mm, n + 1)
                if n >= 2:
                    dve.wait_ge(pv_mm, n - 1)
                dve.tensor_tensor(v_att[:, n % 2, :], bank[0:L, 6, :], att_bias[0:L, 0, :], ALU.add)\
                   .then_inc(va_done, 1)

            def scores_masked(n):
                dve.wait_ge(s_mm, n + 1)
                if n >= 2:
                    dve.wait_ge(pt_mm, 2 * n - 2)
                s = probs[:, n % 2, :].rearrange("l (j g s) -> l j g s", j=4, g=G4)
                dve.tensor_tensor(s, bank[0:L, 0:4, 0:G4 * L].rearrange("l j (g s) -> l j g s", g=G4),
                                  bc(causal[:].unsqueeze(1).unsqueeze(1), [L, 4, G4, L]), ALU.add)\
                   .then_inc(s_read, 1)

            def scores_max(n):
                dve.wait_ge(s_read, n + 1)
                dve.tensor_reduce(row_max[:, n % 2, :], probs[:, n % 2, :].rearrange("l (h s) -> l h s", s=L),
                                  AX, ALU.max).then_inc(s_max, 1)

            def sums(n):
                dve.wait_ge(s_exp, n + 1)
                link(dve.tensor_reduce(row_sum[:, n % 2, :], probs[:, n % 2, :].rearrange("l (h s) -> l h s", s=L),
                                       AX, ALU.add))
                dve.reciprocal(row_sum[:, n % 2, :], row_sum[:, n % 2, :]).then_inc(s_sum, 1)

            def attended(n):
                dve.wait_ge(pv_mm, n + 1)
                dve.wait_ge(s_sum, n + 1)
                if n:
                    dve.wait_ge(at_mm, n)
                dve.tensor_tensor(o_att[:].rearrange("l (g j d) -> l g j d", g=G4, j=4),
                                  bank[0:L, 7, :].rearrange("l (g j d) -> l g j d", g=G4, j=4),
                                  bc(row_sum[:, n % 2, :].rearrange("l (j g) -> l g j", j=4).unsqueeze(3),
                                     [L, G4, 4, AD]), ALU.mult).then_inc(pv_done, 1)

            def attended_lo(n):
                dve.wait_ge(at_hi, n + 1)
                mine = lambda a: a[:].rearrange("p k (l n) -> p k l n", n=N)[:, :, :, n]
                dve.tensor_tensor(mine(att_lo), bank[:, 7, 0:KD * L].rearrange("p (k c) -> p k c", k=KD),
                                  f(mine(att_hi)), ALU.subtract).then_inc(at_lo, 1)

            scores_masked(0)
            scores_max(0)
            values_biased(0)
            scores_masked(1)
            scores_max(1)
            for n in range(N):
                if n:
                    attended_lo(n - 1)
                sums(n)
                if n + 1 < N:
                    values_biased(n + 1)
                if n + 2 < N:
                    scores_masked(n + 2)
                attended(n)
                if n + 2 < N:
                    scores_max(n + 2)
                if n == N // 2:
                    split_lo(WO)
            attended_lo(N - 1)
            split_lo(FIRST)
            split_lo(FIRST + 1)

            dve.wait_ge(res2, 2)
            for t in range(TILES):
                r = rows(t)
                dve.wait_ge(o2_mm, t + 1)
                ins = dve.tensor_tensor(x[0:r, t, :], bank[0:r, t % 4, :], x[0:r, t, :], ALU.add)
                ins.then_inc(r2_done, 1)
                dve.wait_ge(r2_done, t + 1)
                norm_stats(t, var2)
                if t:
                    norm_apply(t - 1, std2, x2_done)
            norm_apply(TILES - 1, std2, x2_done)

            dve.memset(sel[:, TILES, :], 0.0)
            link(dve.memset(logits[:], 0.0))
            dve.wait_ge(lg_mm, TILES)
            lg = bank[:, 7, 0:TILES * E].rearrange("p (t e) -> p t e", e=E)
            dve.tensor_copy(logits[:, 0:FULL, :], lg[:, 0:FULL, :])
            link(dve.tensor_copy(logits[0:LAST, FULL:, :], lg[0:LAST, FULL:, :]))
            col = lambda a, s=S3: bc(a[:].unsqueeze(2), s)
            link(dve.tensor_reduce(r_col[:], logits[:], AX, ALU.max))
            dve.tensor_tensor(t_a[:], logits[:], col(r_col), ALU.subtract).then_inc(lg_shift, 1)
            dve.wait_ge(lg_exped, 1)
            mine = bc(lg_exp[:].unsqueeze(3), [P, TILES, E, E])
            other = bc(lg_exp[:].unsqueeze(2), [P, TILES, E, E])
            gt4, eq4 = (a[:].rearrange("p t (e o) -> p t e o", e=E) for a in (gt, eq))
            link(dve.tensor_tensor(eq4, other, mine, ALU.is_equal))
            dve.tensor_tensor(gt4, other, mine, ALU.is_gt)
            link(dve.tensor_tensor(eq[:], eq[:], bc(lower[:].rearrange("p e o -> p (e o)").unsqueeze(1),
                                                    [P, TILES, E * E]), ALU.mult))
            link(dve.tensor_tensor(gt[:], gt[:], eq[:], ALU.add))
            link(dve.tensor_reduce(rank[:], gt4, AX, ALU.add))
            dve.scalar_tensor_tensor(sel[:, 0:TILES, :], rank[:], 1.5, bc(valid[:], S3), ALU.is_lt, ALU.mult)\
               .then_inc(sel_done, 1)
            dve.tensor_scalar(pick1[:], rank[:], 0.0, None, ALU.is_equal)
            link(dve.tensor_scalar(pick2[:], rank[:], 1.0, None, ALU.is_equal))
            dve.wait_ge(rank_mm, 1)
            places = bank[:, 6, 0:(TILES + 1) * E].rearrange("p (t e) -> p t e", e=E)
            link(dve.tensor_reduce(m_col[:, 0:1], places[:, TILES, :], AX, ALU.max))
            link(dve.tensor_scalar(m_col[:, 1:2], m_col[:, 0:1], float(CAP), None, ALU.is_gt))
            dve.tensor_scalar(n_blocks[:], m_col[:, 1:2], float(BLOCKS - E), float(E), ALU.mult, ALU.add)\
               .then_inc(blocks_ready, 1)
            dve.tensor_scalar(over[:], places[:, 0:TILES, :], float(CAP), None, ALU.is_ge)
            link(dve.tensor_tensor(place[:], places[:, 0:TILES, :], bc(first_row[:].unsqueeze(1), S3), ALU.add))
            for c in range(2, PASSES):
                link(dve.scalar_tensor_tensor(over[:], places[:, 0:TILES, :], float(c * CAP), over[:],
                                              ALU.is_ge, ALU.add))
            link(dve.scalar_tensor_tensor(place[:], over[:], float((E - 1) * CAP), place[:], ALU.mult, ALU.add))
            dve.tensor_tensor(over[:], place[:], pick1[:], ALU.mult)
            link(dve.tensor_tensor(over2[:], place[:], pick2[:], ALU.mult))
            with nc.allow_low_precision("whole numbers"):
                dve.tensor_reduce(row1[:], over[:], AX, ALU.add)
                dve.tensor_reduce(row2[:], over2[:], AX, ALU.add).then_inc(rows_ready, 1)
            dve.wait_ge(rows_ready, 1)
            link(dve.tensor_reduce(r_col[:], lg_exp[:], AX, ALU.add))
            link(dve.reciprocal(r_col2[:], r_col[:]))
            link(dve.tensor_tensor(prob[:], lg_exp[:], col(r_col2), ALU.mult))
            dve.tensor_tensor(over[:], pick1[:], prob[:], ALU.mult)
            link(dve.tensor_tensor(over2[:], pick2[:], prob[:], ALU.mult))
            dve.tensor_reduce(gate1[:], over[:], AX, ALU.add)
            link(dve.tensor_reduce(gate2[:], over2[:], AX, ALU.add))
            link(dve.tensor_tensor(r_col[:], gate1[:], gate2[:], ALU.add))
            link(dve.reciprocal(r_col2[:], r_col[:]))
            dve.tensor_tensor(gate1[:], gate1[:], r_col2[:], ALU.mult)
            link(dve.tensor_tensor(gate2[:], gate2[:], r_col2[:], ALU.mult))

            def expert_lo(g, j):
                i = FIRST + j
                dve.wait_ge(w_hi, g * PER + (i + 1))
                dve.tensor_tensor(wlo[i % RING][:], raw[i % RING][:], f(whi[i % RING][:]), ALU.subtract)\
                   .then_inc(w_lo, 1)

            def expert(g):
                first = isinstance(g, int)
                for b in range(2):
                    dve.wait_ge(xgt_hi, g * 2 + b + 1)
                    dve.tensor_tensor(xg_lo[:, 2 * b:2 * b + 2, :],
                                      bank[:, 6 + b, :].rearrange("p (k c) -> p k c", k=2),
                                      f(xg_hi[:, 2 * b:2 * b + 2, :]), ALU.subtract).then_inc(xgt_lo, 1)
                expert_lo(g, 2)
                expert_lo(g, 3)
                for q, ahead in ((0, (4,)), (1, (5, 6)), (2, (7, 8)), (3, (9,))):
                    half = q % 2
                    dve.wait_ge(h_act, g * 8 + 2 * q + 2)
                    if not first or q >= 2:
                        dve.wait_ge(g2_mm, g * 4 + (q - 1))
                    dve.tensor_copy(h_hi[:, half, :, :], hidden[:, half, :, :]).then_inc(h_split_hi, 1)
                    dve.wait_ge(h_split_hi, g * 4 + q + 1)
                    dve.tensor_tensor(h_lo[:, half, :, :], hidden[:, half, :, :], f(h_hi[:, half, :, :]),
                                      ALU.subtract).then_inc(h_split, 1)
                    for j in ahead:
                        expert_lo(g, j)

            expert(0)
            blocks = dve.value_load(n_blocks[0:1, 0:1], min_val=E, max_val=BLOCKS)
            with dve.Fori(1, blocks) as g:
                expert(g)

            for t in range(TILES):
                r = rows(t)
                dve.wait_ge(pick_in[t], 32)
                for c, gate in enumerate((gate1, gate2)):
                    link(dve.scalar_tensor_tensor(x[0:r, t, :], picked[0:r, t, c, :], gate[0:r, t:t + 1],
                                                  x[0:r, t, :], ALU.mult, ALU.add))
                norm_stats(t, var3)
                if t:
                    norm_apply(t - 1, std3, out_ready)
            norm_apply(TILES - 1, std3, out_ready)

        @block.tensor
        def _(pe):
            def wh(i, sub=512):
                return (whi[i % RING][:, 0:KD * sub].rearrange("p (k n) -> p k n", k=KD),
                        wlo[i % RING][:, 0:KD * sub].rearrange("p (k n) -> p k n", k=KD))

            def mm3(o, a, b, first, last):
                pe.matmul(o, a[0], b[0], start=first, stop=False)
                pe.matmul(o, a[0], b[1], start=False, stop=False)
                return pe.matmul(o, a[1], b[0], start=False, stop=last)

            xf = (xf_hi, xf_lo)

            def v_tile(g, t):
                idx, r = TILES * g + t, rows(t)
                if idx >= 2:
                    pe.wait_ge(v_biased, idx - 1)
                if g and t == 0:
                    pe.wait_ge(y_gated, 4)
                w = wh(V1 if g else V0)
                for k in range(KD):
                    mm = mm3(bank[0:r, 4 + idx % 2, :], [a[:, k, t * P:t * P + r] for a in xf],
                             [a[:, k, :] for a in w], k == 0, k == KD - 1)
                mm.then_inc(v_mm, 1)

            def u_half(g, n):
                j, hf = n // 2, n % 2
                if 8 * g + n >= 4:
                    pe.wait_ge(u_scaled, 8 * g + n - 3)
                w = wh(U1 if g else U0)
                for k in range(KD):
                    mm = mm3(bank[:, n % 4, 0:HT], [a[:, k, j * P:(j + 1) * P] for a in w],
                             [a[:, k, hf * HT:(hf + 1) * HT] for a in xf], k == 0, k == KD - 1)
                mm.then_inc(u_mm, 1)

            def mix_head(g, j):
                idx = 4 * g + j
                if idx >= 2:
                    pe.wait_ge(y_gated, idx - 1)
                a = 6 if j % 2 == 0 else 4
                for t in range(TILES):
                    r = rows(t)
                    mm = pe.matmul(bank[:, a + t // 4, (t % 4) * P:(t % 4) * P + r],
                                   v_tok[0:r, t, j * P:(j + 1) * P], mix[0:r, 4 * g + j, 0:r],
                                   start=True, stop=True)
                mm.then_inc(y_mm, 1)

            gated = [(gated0_hi, gated0_lo), (gated1_hi, gated1_lo)]

            def project(t, half):
                r = rows(t)
                if half == 0 and t >= 4:
                    pe.wait_ge(r1_done, t - 3)
                w = wh(O1 if half else O0)
                for k in range(KD):
                    mm = mm3(bank[0:r, t % 4, :], [a[:, k, t * P:t * P + r] for a in gated[half]],
                             [a[:, k, :] for a in w], half == 0 and k == 0, half == 1 and k == KD - 1)
                if half:
                    mm.then_inc(o_mm, 1)

            pe.wait_ge(xf_lo_done, 1)
            pe.wait_ge(w_lo, V0 + 1)
            v_tile(0, 0)
            v_tile(0, 1)
            pe.wait_ge(consts, 13)
            pe.wait_ge(sq_done, 2)
            for t in range(TILES):
                r = rows(t)
                for k in range(KD):
                    mm = pe.matmul(bank[0:r, 2, t:t + 1], squares[:, k, t * P:t * P + r], ones[:, 0:1],
                                   start=(k == 0), stop=(k == KD - 1))
            mm.then_inc(ssq_mm, 1)
            for hf in range(2):
                for k in range(KD):
                    mm = pe.matmul(bank[:, hf, 0:HT], ones[:], squares[:, k, hf * HT:(hf + 1) * HT],
                                   start=(k == 0), stop=(k == KD - 1))
                mm.then_inc(ssq_mm, 1)
            pe.wait_ge(xf_lo_done, 2)
            for t in range(2, TILES):
                v_tile(0, t)
            pe.wait_ge(w_lo, U0 + 1)
            pe.wait_ge(rms_done, 3)
            for n in range(8):
                u_half(0, n)
            pe.wait_ge(mix_done, 1)
            pe.wait_ge(v_act, TILES)
            mix_head(0, 0)
            mix_head(0, 1)
            pe.wait_ge(w_lo, U1 + 1)
            for j in range(4):
                u_half(1, 2 * j)
                u_half(1, 2 * j + 1)
                if j < 2:
                    mix_head(0, j + 2)
            pe.wait_ge(w_lo, V1 + 1)
            for t in range(TILES):
                v_tile(1, t)
            pe.wait_ge(y_lo, 4)
            pe.wait_ge(w_lo, O0 + 1)
            pe.wait_ge(u_scaled, 16)
            project(0, 0)
            pe.wait_ge(v_act, 2 * TILES)
            mix_head(1, 0)
            mix_head(1, 1)
            project(1, 0)
            mix_head(1, 2)
            project(2, 0)
            mix_head(1, 3)
            project(3, 0)
            pe.wait_ge(y_lo, 8)
            pe.wait_ge(w_lo, O1 + 1)
            for t in range(4):
                project(t, 1)
            for t in range(4, TILES):
                project(t, 0)
                project(t, 1)

            def kq(i, w, src):
                n = i % 8
                j = n % 4
                if i >= 2:
                    pe.wait_ge(kq_done, i - 1)
                for k in range(KD):
                    mm = mm3(bank[:, 6 + i % 2, 0:HT], [a[:, k, j * P:(j + 1) * P] for a in w],
                             [a[:, k, :] for a in src], k == 0, k == KD - 1)
                mm.then_inc(kq_mm, 1)

            ctx = [wh(CTX0, HT), wh(CTX1, HT)]
            for hf in range(2):
                pe.wait_ge(w_lo, (CTX1 if hf else CTX0) + 1)
                for j in range(4):
                    kq(4 * hf + j, wh(WK), ctx[hf])
            for t in range(TILES):
                r = rows(t)
                pe.wait_ge(x1_done, t + 1)
                if t >= 2:
                    pe.wait_ge(x1t_lo, t - 1)
                for k in range(KD):
                    mm = pe.transpose(bank[:, 4 + t % 2, k * P:k * P + r], x[0:r, t, k * P:(k + 1) * P],
                                      ident[0:r, 0:r])
                mm.then_inc(x1t_mm, 1)
            pe.wait_ge(x1t_lo, TILES)
            pe.wait_ge(w_lo, WQ + 1)
            for hf in range(2):
                for j in range(4):
                    kq(8 + 4 * hf + j, wh(WQ), [a[:, :, hf * HT:(hf + 1) * HT] for a in (x1_hi, x1_lo)])

            pe.wait_ge(w_lo, WV + 1)
            pe.wait_ge(kq_done, 16)

            def values(n):
                if n >= 1:
                    pe.wait_ge(va_done, n)
                if n >= 2:
                    pe.wait_ge(pv_mm, n - 1)
                c0 = (n % 4) * L
                for k in range(KD):
                    mm = mm3(bank[0:L, 6, :], [a[:, k, c0:c0 + L] for a in ctx[n // 4]],
                             [a[:, k, :] for a in wh(WV)], k == 0, k == KD - 1)
                mm.then_inc(va_mm, 1)

            def scores(n):
                cols = slice(n * L, (n + 1) * L)
                if n >= 1:
                    pe.wait_ge(s_read, n)
                for g in range(G4):
                    for j in range(4):
                        part = slice(AD * j, AD * (j + 1))
                        mm = pe.matmul(bank[0:L, j, g * L:(g + 1) * L], q_feat[part, g, cols],
                                       k_feat[part, g, cols], start=True, stop=True)
                mm.then_inc(s_mm, 1)

            def probs_turned(n, r):
                if 2 * n + r:
                    pe.wait_ge(pt_done, 2 * n + r)
                for jj in range(2):
                    for g in range(G4):
                        c = ((2 * r + jj) * G4 + g) * L
                        mm = pe.transpose(bank[0:L, 4 + jj, g * L:(g + 1) * L], probs[:, n % 2, c:c + L],
                                          ident[0:L, 0:L])
                mm.then_inc(pt_mm, 1)

            def weighted(n):
                pe.wait_ge(va_done, n + 1)
                pe.wait_ge(pt_done, 2 * n + 2)
                if n:
                    pe.wait_ge(at_lo, n)
                for r in range(2):
                    for jj in range(2):
                        for g in range(G4):
                            h = 4 * g + 2 * r + jj
                            c = (jj * G4 + g) * L
                            mm = pe.matmul(bank[0:L, 7, h * AD:(h + 1) * AD], probs_t[:, n % 2, r, c:c + L],
                                           v_att[:, n % 2, h * AD:(h + 1) * AD], start=True, stop=True)
                mm.then_inc(pv_mm, 1)

            def attended_turned(n):
                pe.wait_ge(pv_done, n + 1)
                for k in range(KD):
                    mm = pe.transpose(bank[:, 7, k * L:(k + 1) * L], o_att[:, k * P:(k + 1) * P],
                                      ident[0:L, 0:L])
                mm.then_inc(at_mm, 1)

            scores(0)
            values(0)
            scores(1)
            for n in range(N):
                pe.wait_ge(s_exp, n + 1)
                probs_turned(n, 0)
                if n:
                    attended_turned(n - 1)
                if n + 1 < N:
                    values(n + 1)
                probs_turned(n, 1)
                if n + 2 < N:
                    scores(n + 2)
                weighted(n)
            attended_turned(N - 1)

            def x2_transpose(t):
                r = rows(t)
                pe.wait_ge(x2_done, t + 1)
                if t >= 2:
                    pe.wait_ge(x2t_done, t - 1)
                for k in range(KD):
                    mm = pe.transpose(bank[:, 4 + t % 2, k * P:k * P + r], x[0:r, t, k * P:(k + 1) * P],
                                      ident[0:r, 0:r])
                mm.then_inc(x2t_mm, 1)

            def route(t):
                r = rows(t)
                pe.wait_ge(x2t_done, t + 1)
                for k in range(KD):
                    mm = pe.matmul(bank[0:r, 7, t * E:(t + 1) * E], x2_feat[:, k, t * P:t * P + r], wr[:, k, :],
                                   start=(k == 0), stop=(k == KD - 1))
                mm.then_inc(lg_mm, 1)

            pe.wait_ge(at_lo, N)
            pe.wait_ge(w_lo, WO + 1)
            pe.wait_ge(s_read, N)
            pe.wait_ge(pt_done, 2 * N)
            for t in range(TILES):
                r = rows(t)
                if t >= 4:
                    pe.wait_ge(r2_done, t - 3)
                for k in range(KD):
                    mm = mm3(bank[0:r, t % 4, :], [a[:, k, t * P:t * P + r] for a in (att_hi, att_lo)],
                             [a[:, k, :] for a in wh(WO)], k == 0, k == KD - 1)
                mm.then_inc(o2_mm, 1)
                if t >= 3:
                    x2_transpose(t - 3)
            for t in range(TILES - 6):
                route(t)
            for t in range(TILES - 3, TILES):
                route(t - 3)
                x2_transpose(t)
            for t in range(TILES - 3, TILES):
                route(t)
            pe.wait_ge(sel_done, 1)
            mm = pe.matmul(bank[:, 6, 0:(TILES + 1) * E], before[:], sel[:].rearrange("p t e -> p (t e)"),
                           start=True, stop=False)
            for t in range(TILES):
                mm = pe.matmul(bank[:, 6, (t + 1) * E:(TILES + 1) * E], ones[:],
                               bc(sel[:, t:t + 1, :], [P, TILES - t, E]), start=False, stop=(t == TILES - 1))
            mm.then_inc(rank_mm, 1)

            def through_w1(g, q):
                i = FIRST + W1_PIECE[q]
                pe.wait_ge(w_lo, g * PER + (i + 1))
                w = wh(i)
                for ft in range(4):
                    b = ft // 2
                    if b * 2 == ft and (q >= 2 or not isinstance(g, int)):
                        pe.wait_ge(h_act, g * 8 + (2 * q + b - 3))
                    for k in range(KD):
                        mm = mm3(bank[:, 2 * (q % 2) + b, (ft % 2) * CAP:(ft % 2 + 1) * CAP],
                                 [a[:, k, ft * P:(ft + 1) * P] for a in w],
                                 [a[:, k, :] for a in (xg_hi, xg_lo)], k == 0, k == KD - 1)
                    if ft % 2:
                        mm.then_inc(g1_mm, 1)

            def through_w2(g, q, back=0):
                i = FIRST + W2_PIECE[q] - PER * back
                pe.wait_ge(w_lo, g * PER + (i + 1))
                pe.wait_ge(h_split, g * 4 + (q + 1 - 4 * back))
                if q == 0 and not isinstance(g, int):
                    pe.wait_ge(y_read, g)
                w = wh(FIRST + W2_PIECE[q])
                for s in range(CT):
                    for ft in range(4):
                        mm = mm3(bank[:, 4 + s, :], [a[:, q % 2, ft, s * P:(s + 1) * P] for a in (h_hi, h_lo)],
                                 [a[:, ft, :] for a in w], q == 0 and ft == 0, q == 3 and ft == 3)
                mm.then_inc(g2_mm, 1)

            def expert(g):
                pe.wait_ge(xg_in, g * 16 + 16)
                for b in range(2):
                    if not isinstance(g, int):
                        pe.wait_ge(xgt_lo, g * 2 + (b - 1))
                    for k in range(2 * b, 2 * b + 2):
                        for s in range(CT):
                            c = (k % 2) * CAP + s * P
                            mm = pe.transpose(bank[:, 6 + b, c:c + P], xg[:, s, k * P:(k + 1) * P], ident[:])
                    mm.then_inc(xgt_mm, 1)
                if not isinstance(g, int):
                    through_w2(g, 3, back=1)
                pe.wait_ge(xgt_lo, g * 2 + 2)
                through_w1(g, 0)
                through_w1(g, 1)
                through_w2(g, 0)
                through_w1(g, 2)
                through_w2(g, 1)
                through_w1(g, 3)
                through_w2(g, 2)

            expert(0)
            blocks = pe.value_load(n_blocks[0:1, 0:1], min_val=E, max_val=BLOCKS)
            with pe.Fori(1, blocks) as g:
                expert(g)
            through_w2(blocks, 3, back=1)


def kernel(x, ctx_1024, L0_attn_key, L0_attn_value, L0_attn_u_w, L0_attn_u_b, L0_attn_v_w, L0_attn_v_b,
           L0_attn_o_w, L0_attn_o_b, L0_attn_pos, L0_attn_zero, L0_attn_neg, L0_xattn_Wq, L0_xattn_bq,
           L0_xattn_Wk, L0_xattn_bk, L0_xattn_Wv, L0_xattn_bv, L0_xattn_Wo, L0_xattn_bo, L0_ffn_W1,
           L0_ffn_W2, L0_ffn_Wr):
    import concourse.bacc as bacc
    from concourse.bass_utils import run_bass_kernel_spmd

    def by_k(m):
        return m.reshape(m.shape[0], -1, P).transpose(2, 1, 0)

    def piece(m):
        return by_k(m).reshape(P, -1)

    x = np.asarray(x)
    xt = x.transpose(1, 0, 2).reshape(T, D)
    u_w, v_w, o_w = np.asarray(L0_attn_u_w), np.asarray(L0_attn_v_w), np.asarray(L0_attn_o_w)
    ctx = np.asarray(ctx_1024)[:, :L].reshape(T, D)
    halves = [by_k(ctx[h * HT:(h + 1) * HT]).reshape(P, KD * HT) for h in range(2)]
    halves = [np.concatenate([h, h[:, :2048 - KD * HT]], 1) for h in halves]
    pieces = np.stack([
        piece(v_w[:512]), piece(u_w[:512]), piece(u_w[512:]), piece(v_w[512:]),
        piece(o_w[:, :512]), piece(o_w[:, 512:]), piece(np.asarray(L0_xattn_Wk)), *halves,
        piece(np.asarray(L0_xattn_Wq)), piece(np.asarray(L0_xattn_Wv)), piece(np.asarray(L0_xattn_Wo))])
    w1 = np.asarray(L0_ffn_W1).reshape(E, 4, 512, KD, P).transpose(0, 1, 4, 3, 2).reshape(E, 4, P, 2048)
    w2 = np.asarray(L0_ffn_W2).reshape(E, D, 4, 4, P).transpose(0, 2, 4, 3, 1).reshape(E, 4, P, 2048)
    ffn = np.stack([(w1 if which == 1 else w2)[:, q] for which, q in ORDER], 1).reshape(E * PER, P, 2048)
    ffn = np.concatenate([ffn, ffn[:EXTRA]], 0)
    a = np.concatenate([np.asarray(L0_attn_neg)[:, :N - 1][:, ::-1], np.asarray(L0_attn_zero),
                        np.asarray(L0_attn_pos)[:, :N - 1]], 1)
    taps = np.tile(np.stack([a[:, N - 1 - j:2 * N - 1 - j] for j in range(N)]).reshape(N, MH * N), (BS, 1))

    def col(b):
        return np.asarray(b).reshape(-1, P).T

    arrays = {
        "x_tok": xt, "x_feat": by_k(xt), "pieces": pieces, "ffn_pieces": ffn,
        "u_b": col(L0_attn_u_b), "v_b": np.asarray(L0_attn_v_b), "o_b": np.asarray(L0_attn_o_b),
        "mix_taps": taps, "bq": col(L0_xattn_bq), "bk": col(L0_xattn_bk),
        "bv_bo": np.stack([np.asarray(L0_xattn_bv), np.asarray(L0_xattn_bo)]),
        "router_w": by_k(np.asarray(L0_ffn_Wr)),
    }
    arrays = {f"in_{k}": np.ascontiguousarray(v) for k, v in arrays.items()}
    nc = bacc.Bacc("TRN2", target_bir_lowering=False, num_devices=1)
    args = [nc.dram_tensor(k, v.shape, F32, kind="ExternalInput").ap() for k, v in arrays.items()]
    out = nc.dram_tensor("out", (T, D), F32, kind="ExternalOutput").ap()
    decoder_layer(nc, *args, out)
    result = run_bass_kernel_spmd(nc, [arrays], core_ids=[0])
    return result.results[0]["out"].reshape(L, N, D).transpose(1, 0, 2)
```

```python
import numpy as np

import concourse.bass as bass
from concourse import mybir

F32 = mybir.dt.float32
F32R = mybir.dt.float32r
I32 = mybir.dt.int32
ALU = mybir.AluOpType
ACT = mybir.ActivationFunctionType
AX = mybir.AxisListType.X

P = 128
N, L, D = 8, 100, 512
T = N * L
HT = T // 2
KD = D // P
TILES = -(-T // P)
FULL = T // P
LAST = T - FULL * P
F1 = 2 * D
MH = F1 // P
BS = P // N
AH, AD = 16, 32
HB = AH * L // 2
G4 = AH // 4
E, DFF = 8, 2048
CAP = 256
CT = CAP // P
PASSES = -(-T // CAP)
BLOCKS = PASSES * E
RING = 4
EPS = 1e-5
MASKED = -1e30

V0, U0, U1, V1, O0, O1, WK, CTX0, CTX1, WQ, WV, WO = range(12)
FIRST = 12
ORDER = [(1, 0), (1, 1), (2, 0), (1, 2), (2, 1), (1, 3), (2, 2), (2, 3)]
PER = len(ORDER)
W1_PIECE = [ORDER.index((1, q)) for q in range(4)]
W2_PIECE = [ORDER.index((2, q)) for q in range(4)]
EXTRA = 2


def rows(t):
    return min(P, T - t * P)


def decoder_layer(nc, x_tok, x_feat, pieces, ffn_pieces, u_b, v_b, o_b, mix_taps, bq, bk, bv_bo,
                  router_w, out):
    routed = nc.dram_tensor("routed", (BLOCKS * CAP, D), F32, kind="Internal").ap()
    expert_out = nc.dram_tensor("expert_out", (BLOCKS * CAP, D), F32, kind="Internal").ap()

    top = [-(-nc.sbuf_base // 64) * 64]

    def sb(name, shape, dt=F32, offset=None):
        if offset is None:
            offset = top[0]
            top[0] += -(-int(np.prod(shape[1:])) * 4 // 32) * 32
        return nc.alloc_sbuf_tensor_at(name, list(shape), dt, offset=offset)

    FEAT = KD * T * 4
    raw = [sb(f"raw{i}", [P, 2048]) for i in range(RING)]
    whi = [sb(f"whi{i}", [P, 2048], F32R) for i in range(RING)]
    wlo = [sb(f"wlo{i}", [P, 2048], F32R) for i in range(RING)]
    region_a = top[0]
    xf_hi = sb("xf_hi", [P, KD, T], F32R)
    xf_lo = sb("xf_lo", [P, KD, T], F32R)
    region_b = top[0]
    gated0_hi = sb("gated0_hi", [P, KD, T], F32R)
    gated0_lo = sb("gated0_lo", [P, KD, T], F32R)
    region_c = top[0]
    u_feat = sb("u_feat", [P, KD, T])
    v_tok = sb("v_tok", [P, TILES, 512])
    x = sb("x", [P, TILES, D])
    gated1_hi = sb("gated1_hi", [P, KD, T], F32R, region_a)
    gated1_lo = sb("gated1_lo", [P, KD, T], F32R, region_a + FEAT)
    k_feat = sb("k_feat", [P, KD, T], F32, region_a)
    q_feat = sb("q_feat", [P, KD, T], F32, region_a + FEAT)
    x2_feat = sb("x2_feat", [P, KD, T], F32, region_a)
    squares = sb("squares", [P, TILES, D], F32, region_b)
    diag = sb("diag", [P, T], F32, region_b + TILES * D * 4)
    probs = sb("probs", [L, 2, AH * L], F32, region_b)
    probs_t = sb("probs_t", [L, 2, 2, HB], F32, region_b + 2 * AH * L * 4)
    x_f = sb("x_f", [P, KD, T], F32, region_c)
    x1_hi = sb("x1_hi", [P, KD, T], F32R, region_c)
    x1_lo = sb("x1_lo", [P, KD, T], F32R, region_c + FEAT)
    att_hi = sb("att_hi", [P, KD, T], F32R, region_c)
    att_lo = sb("att_lo", [P, KD, T], F32R, region_c + FEAT)
    moe_top = [region_a]

    def sb_moe(name, shape, dt=F32):
        o = moe_top[0]
        moe_top[0] += int(np.prod(shape[1:])) * 4
        assert moe_top[0] <= region_c
        return sb(name, shape, dt, o)

    xg = sb_moe("xg", [P, CT, D])
    xg_hi = sb_moe("xg_hi", [P, KD, CAP], F32R)
    xg_lo = sb_moe("xg_lo", [P, KD, CAP], F32R)
    hidden = sb_moe("hidden", [P, 2, 4, CAP])
    h_hi = sb_moe("h_hi", [P, 2, 4, CAP], F32R)
    h_lo = sb_moe("h_lo", [P, 2, 4, CAP], F32R)
    y_sb = sb_moe("y_sb", [P, CT, D])
    picked = sb("picked", [P, TILES, 2, D], F32, region_a)
    x2_hi = sb("x2_hi", [P, TILES, D], F32R, region_a + FEAT)
    x2_lo = sb("x2_lo", [P, TILES, D], F32R, region_a + FEAT + TILES * D * 4)
    slot0 = sb("slot0", [P, TILES, CAP], F32R, region_a + FEAT + 2 * TILES * D * 4)
    assert region_a + FEAT + (2 * D + CAP) * TILES * 4 <= region_c

    v_bias_at = top[0]
    v_bias = sb("v_bias", [P, F1])
    att_bias = sb("att_bias", [P, 2, D], F32, v_bias_at)
    mix_at = top[0]
    mix = sb("mix", [P, MH, P])
    v_att = sb("v_att", [L, 2, D], F32, mix_at)
    o_bias = sb("o_bias", [P, D])
    ident = sb("ident", [P, P])
    ones_r = sb("ones_r", [P, P], F32R)
    before_r = sb("before_r", [P, P], F32R)
    ones = sb("ones", [P, P])
    before = sb("before", [P, P])
    scale_row = sb("scale_row", [P, T])
    scale_col = sb("scale_col", [P, TILES])
    causal = sb("causal", [L, L])
    zeros = sb("zeros", [P, D])
    taps = sb("taps", [P, MH * N])
    same_b = sb("same_b", [P, BS])
    ub_col = sb("ub_col", [P, MH])
    bq_col = sb("bq_col", [P, KD])
    bk_col = sb("bk_col", [P, KD])
    eps_col = sb("eps_col", [P, 1])
    wr = sb("wr", [P, KD, E])
    lower = sb("lower", [P, E, E])
    first_row = sb("first_row", [P, E])
    valid = sb("valid", [P, TILES, 1])
    bn = sb("bn", [P, 2, 6])
    mv = sb("mv", [P, 2, 2])
    std = sb("std", [P, 2])
    rstd = sb("rstd", [P, 2])
    shift = sb("shift", [P, 2])
    row_max = sb("row_max", [L, 2, AH])
    row_sum = sb("row_sum", [L, 2, AH])
    slots = sb("slots", [P, CAP])
    n_blocks = sb("n_blocks", [P, 1], I32)
    row1 = sb("row1", [P, TILES], I32)
    row2 = sb("row2", [P, TILES], I32)
    gate1 = sb("gate1", [P, TILES])
    gate2 = sb("gate2", [P, TILES])
    assert top[0] <= nc.sbuf_usable_end, top[0]
    router_top = [region_c]

    def sb_router(name, shape, dt=F32):
        o = router_top[0]
        router_top[0] += -(-int(np.prod(shape[1:])) * 4 // 32) * 32
        assert router_top[0] <= region_c + 2 * FEAT
        return sb(name, shape, dt, o)

    S3 = [P, TILES, E]
    logits = sb_router("logits", S3)
    lg_exp = sb_router("lg_exp", S3)
    prob = sb_router("prob", S3)
    t_a = sb_router("t_a", S3)
    rank = sb_router("rank", S3)
    pick1 = sb_router("pick1", S3)
    pick2 = sb_router("pick2", S3)
    sel = sb_router("sel", [P, TILES + 1, E], F32R)
    place = sb_router("place", S3)
    over = sb_router("over", S3)
    over2 = sb_router("over2", S3)
    gt = sb_router("gt", [P, TILES, E * E])
    eq = sb_router("eq", [P, TILES, E * E])
    r_col = sb_router("r_col", [P, TILES])
    r_col2 = sb_router("r_col2", [P, TILES])
    m_col = sb_router("m_col", [P, 4])
    place0 = sb_router("place0", [P, TILES])

    bank = nc.alloc_psum_tensor("bank", [P, 8, 512], F32)

    def sem(name):
        return nc.alloc_semaphore(name)

    x_in, small_in, o_bias_in, bias2_in = sem("x_in"), sem("small_in"), sem("o_bias_in"), sem("bias2_in")
    xt_in = [sem(f"xt_in{hf}") for hf in range(2)]
    consts = sem("consts")
    w_in = [sem(f"w_in{i}") for i in range(RING)]
    w_hi, w_lo = sem("w_hi"), sem("w_lo")
    sq_done, rms_done, diag_done = sem("sq_done"), sem("rms_done"), sem("diag_done")
    scale_mm, scale_row_done = sem("scale_mm"), sem("scale_row_done")
    xf_hi_done, xf_lo_done, mix_done = sem("xf_hi_done"), sem("xf_lo_done"), sem("mix_done")
    u_mm, u_scaled, u_act = sem("u_mm"), sem("u_scaled"), sem("u_act")
    v_mm, v_biased, v_act = sem("v_mm"), sem("v_biased"), sem("v_act")
    y_mm, y_gated, y_hi, y_lo = sem("y_mm"), sem("y_gated"), sem("y_hi"), sem("y_lo")
    res1 = sem("res1")
    o_mm, r1_done, var1, std1, x1_done = sem("o_mm"), sem("r1_done"), sem("var1"), sem("std1"), sem("x1_done")
    x1t_mm, x1t_hi, x1t_lo = sem("x1t_mm"), sem("x1t_hi"), sem("x1t_lo")
    kq_mm, kq_done = sem("kq_mm"), sem("kq_done")
    res2 = sem("res2")
    va_mm, va_done = sem("va_mm"), sem("va_done")
    s_mm, s_read, s_max, s_sub, s_exp, s_total = (sem(s) for s in
                                                ("s_mm", "s_read", "s_max", "s_sub", "s_exp", "s_total"))
    s_norm = [sem(f"s_norm{r}") for r in range(2)]
    pt_mm, pt_done, pv_mm = sem("pt_mm"), sem("pt_done"), sem("pv_mm")
    at_hi, at_lo = sem("at_hi"), sem("at_lo")
    o2_mm, r2_done, var2, std2, x2_done = sem("o2_mm"), sem("r2_done"), sem("var2"), sem("std2"), sem("x2_done")
    x2t_mm, x2t_done, lg_mm = sem("x2t_mm"), sem("x2t_done"), sem("lg_mm")
    lg_shift, lg_exped, sel_done, rank_mm = sem("lg_shift"), sem("lg_exped"), sem("sel_done"), sem("rank_mm")
    slot_done, x2_hi_done, x2_lo_done = sem("slot_done"), sem("x2_hi_done"), sem("x2_lo_done")
    rows_ready, blocks_ready = sem("rows_ready"), sem("blocks_ready")
    zero_set, zeroed, scattered = sem("zero_set"), sem("zeroed"), sem("scattered")
    block_begun = sem("block_begun")
    defined, all_out = sem("defined"), sem("all_out")
    xg_in = sem("xg_in")
    xgt_mm, xgt_hi, xgt_lo = sem("xgt_mm"), sem("xgt_hi"), sem("xgt_lo")
    g1_mm, h_act, h_split_hi, h_split = sem("g1_mm"), sem("h_act"), sem("h_split_hi"), sem("h_split")
    g2_mm, y_read, y_out = sem("g2_mm"), sem("y_read"), sem("y_out")
    pick_in = [[sem(f"pick_in{t}_{c}") for c in range(2)] for t in range(TILES)]
    norm2, norm3 = sem("norm2"), sem("norm3")
    var3, std3, out_ready, out_done = sem("var3"), sem("std3"), sem("out_ready"), sem("out_done")
    dve_step = sem("dve_step")

    def released(i):
        if i < FIRST:
            return {U0: (u_mm, 8), V0: (v_mm, TILES), U1: (u_mm, 16), V1: (v_mm, 2 * TILES),
                    O0: (o_mm, TILES), O1: (o_mm, TILES), WK: (kq_mm, 8), CTX0: (va_mm, N // 2),
                    CTX1: (va_mm, N), WQ: (kq_mm, 16), WV: (va_mm, N), WO: (o2_mm, TILES)}[i]
        return expert_piece_released(0, i - FIRST)

    def expert_piece_released(g, j):
        back = 1 if isinstance(j, int) and j < 0 else 0
        which, q = ORDER[j % PER]
        if which == 1:
            return g1_mm, (g - back) * 8 + 2 * q + 2
        return g2_mm, (g - back) * 4 + q + 1

    bc = lambda ap, shape: ap.broadcast_to(list(shape))

    def heads8(a, n, r):
        return a[:, n % 2, r * HB:(r + 1) * HB].rearrange("l (h s) -> l h s", s=L)

    with nc.Block() as block:

        @block.sync
        def _(sp):
            def load_piece(i):
                if i >= RING:
                    sp.wait_ge(w_lo, i - RING + 1)
                src = pieces[i] if i < FIRST else ffn_pieces[i - FIRST]
                sp.dma_start(raw[i % RING][:], src).then_inc(w_in[i % RING], 16)

            def load_x(hf):
                sp.dma_start(x_f[:, :, hf * HT:(hf + 1) * HT], x_feat[:, :, hf * HT:(hf + 1) * HT])\
                  .then_inc(xt_in[hf], 16)

            load_x(0)
            load_piece(V0)
            load_x(1)
            sp.dma_start(x[:, 0:FULL, :], x_tok[0:FULL * P].rearrange("(t p) d -> p t d", p=P)).then_inc(x_in, 16)
            sp.dma_start(x[0:LAST, FULL, :], x_tok[FULL * P:T]).then_inc(x_in, 16)
            load_piece(U0)
            sp.dma_start(v_bias[:], v_b.partition_broadcast(P)).then_inc(small_in, 16)
            sp.dma_start(ub_col[:], u_b).then_inc(small_in, 16)
            sp.dma_start(taps[:], mix_taps).then_inc(small_in, 16)
            sp.dma_start(bq_col[:], bq).then_inc(small_in, 16)
            sp.dma_start(bk_col[:], bk).then_inc(small_in, 16)
            sp.dma_start(wr[:], router_w).then_inc(small_in, 16)
            load_piece(U1)
            load_piece(V1)
            sp.dma_start(o_bias[:], o_b.partition_broadcast(P)).then_inc(o_bias_in, 16)
            load_piece(O0)
            sp.wait_ge(zero_set, 1)
            for g in range(E):
                sp.dma_start(routed[g * CAP:(g + 1) * CAP].rearrange("(n p) d -> p n d", p=P),
                             bc(zeros[:].unsqueeze(1), [P, CT, D])).then_inc(zeroed, 16)
            load_piece(O1)
            load_piece(WK)
            load_piece(CTX0)
            sp.wait_ge(v_biased, 2 * TILES)
            sp.dma_start(att_bias[:], bv_bo.partition_broadcast(P)).then_inc(bias2_in, 16)
            for i in range(CTX1, FIRST + 2):
                load_piece(i)

            def load_expert_pieces(g):
                for j in range(EXTRA, PER + EXTRA):
                    i = FIRST + j
                    sp.wait_ge(w_lo, g * PER + (i - RING + 1))
                    if j == EXTRA:
                        sp.sem_inc(block_begun, 1)
                    src = ffn_pieces[bass.ds((g & (E - 1)) * PER + j, 1)].rearrange("a p n -> (a p) n")
                    sp.dma_start(raw[i % RING][:], src).then_inc(w_in[i % RING], 16)

            for j in range(EXTRA, RING):
                i = FIRST + j
                sp.wait_ge(w_lo, i - RING + 1)
                sp.dma_start(raw[i % RING][:], ffn_pieces[j]).then_inc(w_in[i % RING], 16)
            sp.wait_ge(blocks_ready, 1)
            blocks = sp.value_load(n_blocks[0:1, 0:1], min_val=E, max_val=BLOCKS)
            sp.wait_ge(zeroed, 16 * E)
            with sp.Fori(E - 1, blocks) as g:
                sp.dma_start(routed[bass.ds(g * CAP, CAP)].rearrange("(n p) d -> p n d", p=P),
                             bc(zeros[:].unsqueeze(1), [P, CT, D])).then_inc(zeroed, 16)
            for j in range(RING, PER + EXTRA):
                i = FIRST + j
                sp.wait_ge(w_lo, i - RING + 1)
                sp.dma_start(raw[i % RING][:], ffn_pieces[j]).then_inc(w_in[i % RING], 16)
            with sp.Fori(1, blocks) as g:
                load_expert_pieces(g)
            for t in range(TILES):
                sp.wait_ge(out_ready, t + 1)
                sp.dma_start(out[t * P:t * P + rows(t)], x[0:rows(t), t, :]).then_inc(out_done, 16)
            sp.wait_ge(out_done, 16 * TILES)

        @block.gpsimd
        def _(pool):
            pool.memset(ident[:], 0.0).then_inc(consts, 1)
            pool.memset(ones[:], 1.0).then_inc(consts, 1)
            pool.memset(before[:], 1.0).then_inc(consts, 1)
            pool.memset(causal[:], 0.0).then_inc(consts, 1)
            pool.memset(lower[:], 1.0).then_inc(consts, 1)
            pool.memset(valid[:], 1.0).then_inc(consts, 1)
            pool.memset(eps_col[:], EPS).then_inc(consts, 1)
            pool.memset(scale_col[:], 0.0).then_inc(consts, 1)
            pool.iota(first_row[:], [[CAP, E]], base=0, channel_multiplier=0,
                      allow_small_or_imprecise_dtypes=True).then_inc(consts, 1)
            pool.iota(slots[:], [[1, CAP]], base=1, channel_multiplier=0,
                      allow_small_or_imprecise_dtypes=True).then_inc(consts, 1)
            pool.wait_ge(consts, 10)
            pool.affine_select(out=ident[:], in_=ident[:], compare_op=ALU.not_equal, fill=1.0, base=0,
                               pattern=[[-1, P]], channel_multiplier=1).then_inc(consts, 1)
            pool.affine_select(out=before[:], in_=before[:], compare_op=ALU.is_gt, fill=0.0, base=0,
                               pattern=[[1, P]], channel_multiplier=-1).then_inc(consts, 1)
            pool.affine_select(out=causal[:], in_=causal[:], compare_op=ALU.is_ge, fill=MASKED, base=0,
                               pattern=[[-1, L]], channel_multiplier=1).then_inc(consts, 1)
            pool.affine_select(out=lower[:], in_=lower[:], compare_op=ALU.is_gt, fill=0.0, base=0,
                               pattern=[[1, E], [-1, E]], channel_multiplier=0).then_inc(consts, 1)
            pool.affine_select(out=valid[:, :, 0], in_=valid[:, :, 0], compare_op=ALU.is_ge, fill=0.0,
                               base=T - 1, pattern=[[-P, TILES]], channel_multiplier=-1).then_inc(consts, 1)
            pool.memset(zeros[:], 0.0).then_inc(zero_set, 1)

            pool.wait_ge(sq_done, TILES)
            for r, ts in ((P, slice(0, FULL)), (LAST, slice(FULL, TILES))):
                a = x[0:r, ts, :]
                pool.tensor_tensor(a, a, a, ALU.add).then_inc(res1, 1)
            pool.wait_ge(res1, 2)
            pool.wait_ge(o_bias_in, 16)
            for r, ts in ((P, slice(0, FULL)), (LAST, slice(FULL, TILES))):
                a = x[0:r, ts, :]
                pool.tensor_tensor(a, a, bc(o_bias[0:r].unsqueeze(1), a.shape), ALU.add).then_inc(res1, 1)
            pool.wait_ge(bias2_in, 16)
            pool.wait_ge(x1t_mm, TILES)
            for r, ts in ((P, slice(0, FULL)), (LAST, slice(FULL, TILES))):
                a = x[0:r, ts, :]
                pool.tensor_tensor(a, a, bc(att_bias[0:r, 1:2, :], a.shape), ALU.add).then_inc(res2, 1)
            for n in range(N):
                for r in range(2):
                    pool.wait_ge(s_max, 2 * n + r + 1)
                    s = heads8(probs, n, r)
                    pool.tensor_tensor(s, s, bc(row_max[:, n % 2, 8 * r:8 * r + 8].unsqueeze(2), [L, 8, L]),
                                       ALU.subtract).then_inc(s_sub, 1)
                pool.wait_ge(s_total, n + 1)
                pool.tensor_tensor(s, s, bc(row_sum[:, n % 2, 8:16].unsqueeze(2), [L, 8, L]), ALU.mult)\
                    .then_inc(s_norm[1], 1)

            pool.wait_ge(w_lo, WO)
            for i in (WO, FIRST, FIRST + 1):
                pool.wait_ge(w_hi, i + 1)
                pool.tensor_tensor(wlo[i % RING][:], raw[i % RING][:], whi[i % RING][:].bitcast(F32), ALU.subtract)\
                    .then_inc(w_lo, 1)
            for t in range(TILES):
                r = rows(t)
                pool.wait_ge(x2_hi_done, t + 1)
                pool.tensor_tensor(x2_lo[0:r, t, :], x[0:r, t, :], x2_hi[0:r, t, :].bitcast(F32), ALU.subtract)\
                    .then_inc(x2_lo_done, 1)

            pool.wait_ge(blocks_ready, 1)
            blocks = pool.value_load(n_blocks[0:1, 0:1], min_val=E, max_val=BLOCKS)
            pool.wait_ge(rows_ready, 1)
            pool.wait_ge(zeroed, blocks * 16 + 16)
            pool.sem_inc(defined, 1)
            pool.wait_ge(defined, 1)
            for t in range(TILES):
                for to in (row1, row2):
                    pool.indirect_dma_start(
                        out=routed, out_offset=bass.IndirectOffsetOnAxis(ap=to[0:rows(t), t:t + 1], axis=0),
                        in_=x[0:rows(t), t, :], in_offset=None).then_inc(scattered, 16)
            pool.wait_ge(scattered, 32 * TILES)
            with pool.Fori(1, blocks) as g:
                pool.wait_ge(xgt_mm, g * 2)
                pool.dma_start(xg[:], routed[bass.ds(g * CAP, CAP)].rearrange("(s p) d -> p s d", p=P))\
                    .then_inc(xg_in, 16)
            pool.wait_ge(y_out, blocks * 16)
            pool.sem_inc(all_out, 1)
            pool.wait_ge(all_out, 1)
            def pick(written):
                for t in range(TILES):
                    for c, frm in enumerate((row1, row2)):
                        pool.indirect_dma_start(
                            out=picked[0:rows(t), t, c, :], out_offset=None, in_=written,
                            in_offset=bass.IndirectOffsetOnAxis(ap=frm[0:rows(t), t:t + 1], axis=0))\
                            .then_inc(pick_in[t][c], 16)

            with pool.If(blocks < E + 1):
                pick(expert_out[0:E * CAP])
            with pool.Else():
                pick(expert_out)

        @block.scalar
        def _(act):
            def split_hi(i):
                act.wait_ge(w_in[i % RING], 16 * (i // RING + 1))
                if i >= RING:
                    act.wait_ge(*released(i - RING))
                act.activation(whi[i % RING][:], raw[i % RING][:], ACT.Copy).then_inc(w_hi, 1)

            def x_hi(hf):
                cols = slice(hf * HT, (hf + 1) * HT)
                act.wait_ge(xt_in[hf], 16)
                act.activation(xf_hi[:, :, cols], x_f[:, :, cols], ACT.Copy).then_inc(xf_hi_done, 1)

            def v_silu(g, t):
                act.wait_ge(v_biased, TILES * g + t + 1)
                act.activation(v_tok[0:rows(t), t, :], v_tok[0:rows(t), t, :], ACT.Silu).then_inc(v_act, 1)

            def u_silu(g, n):
                j, hf = n // 2, n % 2
                a = u_feat[:, j, hf * HT:(hf + 1) * HT]
                act.wait_ge(u_scaled, 8 * g + n + 1)
                act.activation(a, a, ACT.Silu, bias=ub_col[:, 4 * g + j:4 * g + j + 1]).then_inc(u_act, 1)

            def gated_hi(g, j):
                act.wait_ge(y_gated, 4 * g + j + 1)
                act.activation((gated1_hi if g else gated0_hi)[:, j, :], u_feat[:, j, :], ACT.Copy)\
                   .then_inc(y_hi, 1)

            x_hi(0)
            split_hi(V0)
            x_hi(1)
            act.wait_ge(consts, 15)
            act.wait_ge(x_in, 32)
            for t in range(TILES):
                r = rows(t)
                act.activation(squares[0:r, t, :], x[0:r, t, :], ACT.Square, accum_out=scale_col[0:r, t:t + 1])\
                   .then_inc(sq_done, 1)
            act.wait_ge(sq_done, TILES)
            act.activation(scale_col[:], scale_col[:], ACT.Sqrt, scale=1.0 / D)\
               .then_inc(rms_done, 1)
            split_hi(U0)
            for t in range(3):
                v_silu(0, t)
            split_hi(U1)
            for t in range(3, TILES):
                v_silu(0, t)
            for hf in range(2):
                act.wait_ge(scale_mm, hf + 1)
                act.activation(scale_row[:, hf * HT:(hf + 1) * HT], bank[:, 2 + hf, 0:HT], ACT.Copy)\
                   .then_inc(scale_row_done, 1)
            split_hi(V1)
            act.wait_ge(small_in, 96)
            for n in range(8):
                u_silu(0, n)
            gated_hi(0, 0)
            for j in range(4):
                if j < 3:
                    gated_hi(0, j + 1)
                u_silu(1, 2 * j)
                u_silu(1, 2 * j + 1)
                if j in (0, 2):
                    split_hi(O1 if j else O0)
            split_hi(WK)
            for t in range(TILES):
                v_silu(1, t)
            split_hi(CTX0)
            for j in range(4):
                gated_hi(1, j)

            act.wait_ge(consts, 15)
            for t in range(TILES):
                r = rows(t)
                act.wait_ge(var1, t + 1)
                act.activation(std[0:r, t % 2:t % 2 + 1], mv[0:r, t % 2, 1:2], ACT.Sqrt,
                               bias=eps_col[0:r, :]).then_inc(std1, 1)
            split_hi(CTX1)

            def kq(i):
                c, n = divmod(i, 8)
                j, hf = (n % 4, n // 4)
                act.wait_ge(kq_mm, i + 1)
                to, frm = k_feat[:, j, hf * HT:(hf + 1) * HT], bank[:, 6 + i % 2, 0:HT]
                if c:
                    to = q_feat[:, j, :].rearrange("p (n l) -> p n l", n=N)[:, :, hf * L // 2:(hf + 1) * L // 2]
                    frm = frm.rearrange("p (l n) -> p n l", n=N)
                act.activation(to, frm, ACT.Identity, bias=(bq_col if c else bk_col)[:, j:j + 1])\
                   .then_inc(kq_done, 1)

            for i in range(8):
                kq(i)
                if i < TILES:
                    r = rows(i)
                    act.wait_ge(x1t_mm, i + 1)
                    act.activation(x1_hi[:, :, i * P:i * P + r],
                                   bank[:, 4 + i % 2, :].rearrange("p (k c) -> p k c", k=KD)[:, :, 0:r],
                                   ACT.Copy).then_inc(x1t_hi, 1)
                if i == 2:
                    split_hi(WQ)
            split_hi(WV)
            for i in range(8, 16):
                kq(i)

            def exp_of(n, r):
                act.wait_ge(s_sub, 2 * n + r + 1)
                act.activation(heads8(probs, n, r), heads8(probs, n, r), ACT.Exp, scale=float(AD) ** -0.5)\
                   .then_inc(s_exp, 1)

            def turned(n, r):
                act.wait_ge(pt_mm, 2 * n + r + 1)
                if n >= 2:
                    act.wait_ge(pv_mm, n - 1)
                act.activation(probs_t[:, n % 2, r, :].rearrange("s (j c) -> s j c", j=2),
                               bank[0:L, 4:6, 0:G4 * L], ACT.Copy).then_inc(pt_done, 1)

            def attended_hi(n):
                act.wait_ge(pv_mm, n + 1)
                act.activation(att_hi[:].rearrange("p k (l n) -> p k l n", n=N)[:, :, :, n],
                               bank[:, 7, 0:KD * L].rearrange("p (k c) -> p k c", k=KD), ACT.Copy)\
                   .then_inc(at_hi, 1)

            exp_of(0, 0)
            exp_of(0, 1)
            turned(0, 0)
            exp_of(1, 0)
            exp_of(1, 1)
            for n in range(N):
                turned(n, 1)
                attended_hi(n)
                if n + 1 < N:
                    turned(n + 1, 0)
                if n + 2 < N:
                    exp_of(n + 2, 0)
                    exp_of(n + 2, 1)
                if n == N // 2:
                    split_hi(WO)
            split_hi(FIRST)
            split_hi(FIRST + 1)

            def x2_out_of_psum(t):
                r = rows(t)
                act.wait_ge(x2t_mm, t + 1)
                act.activation(x2_feat[:, :, t * P:t * P + r],
                               bank[:, 4 + t % 2, :].rearrange("p (k c) -> p k c", k=KD)[:, :, 0:r],
                               ACT.Copy).then_inc(x2t_done, 1)

            def normalise(t, factors, done):
                r, b = rows(t), t % 2
                act.wait_ge(factors, t + 1)
                act.activation(x[0:r, t, :], x[0:r, t, :], ACT.Identity, bias=shift[0:r, b:b + 1],
                               scale=rstd[0:r, b:b + 1]).then_inc(done, 1)

            def x2_halves(t):
                x2_out_of_psum(t)
                act.activation(x2_hi[0:rows(t), t, :], x[0:rows(t), t, :], ACT.Copy).then_inc(x2_hi_done, 1)

            for t in range(TILES):
                r = rows(t)
                act.wait_ge(var2, t + 1)
                act.activation(std[0:r, t % 2:t % 2 + 1], mv[0:r, t % 2, 1:2], ACT.Sqrt,
                               bias=eps_col[0:r, :]).then_inc(std2, 1)
                if t:
                    normalise(t - 1, norm2, x2_done)
                if t >= 2:
                    x2_halves(t - 2)
            normalise(TILES - 1, norm2, x2_done)
            x2_halves(TILES - 2)
            x2_halves(TILES - 1)
            act.wait_ge(lg_shift, 1)
            act.activation(lg_exp[:], t_a[:], ACT.Exp).then_inc(lg_exped, 1)

            def expert_hi(g, j):
                i = FIRST + j
                act.wait_ge(w_in[i % RING], (g * 2 + (i // RING + 1)) * 16)
                if j >= RING or not isinstance(g, int):
                    act.wait_ge(*expert_piece_released(g, j - RING))
                else:
                    act.wait_ge(*released(i - RING))
                act.activation(whi[i % RING][:], raw[i % RING][:], ACT.Copy).then_inc(w_hi, 1)

            def expert(g):
                first = isinstance(g, int)
                for b in range(2):
                    act.wait_ge(xgt_mm, g * 2 + b + 1)
                    act.activation(xg_hi[:, 2 * b:2 * b + 2, :],
                                   bank[:, 6 + b, :].rearrange("p (k c) -> p k c", k=2), ACT.Copy)\
                       .then_inc(xgt_hi, 1)
                expert_hi(g, 2)
                if not first:
                    results(g)
                expert_hi(g, 3)
                for q, ahead in ((0, (4,)), (1, (5, 6)), (2, (7, 8)), (3, (9,))):
                    for b in range(2):
                        act.wait_ge(g1_mm, g * 8 + (2 * q + b + 1))
                        if not first or q >= 2:
                            act.wait_ge(h_split, g * 4 + (q - 1))
                        act.activation(hidden[:, q % 2, 2 * b:2 * b + 2, :],
                                       bank[:, 2 * (q % 2) + b, :].rearrange("p (f c) -> p f c", f=2),
                                       ACT.Silu).then_inc(h_act, 1)
                    for j in ahead:
                        expert_hi(g, j)

            def results(g):
                act.wait_ge(g2_mm, g * 4)
                act.activation(y_sb[:], bank[:, 4:6, :], ACT.Copy).then_inc(y_read, 1)
                act.wait_ge(y_read, g)
                act.dma_start(expert_out[bass.ds((g - 1) * CAP, CAP)].rearrange("(s p) d -> p s d", p=P),
                              y_sb[:]).then_inc(y_out, 16)

            expert(0)
            blocks = act.value_load(n_blocks[0:1, 0:1], min_val=E, max_val=BLOCKS)
            with act.Fori(1, blocks) as g:
                expert(g)
                act.wait_ge(y_out, g * 16)
            results(blocks)
            for t in range(TILES):
                r = rows(t)
                act.wait_ge(var3, t + 1)
                act.activation(std[0:r, t % 2:t % 2 + 1], mv[0:r, t % 2, 1:2], ACT.Sqrt,
                               bias=eps_col[0:r, :]).then_inc(std3, 1)
                if t:
                    normalise(t - 1, norm3, out_ready)
            normalise(TILES - 1, norm3, out_ready)

        @block.vector
        def _(dve):
            steps = [0]

            def link(ins):
                steps[0] += 1
                ins.then_inc(dve_step, 1)
                dve.wait_ge(dve_step, steps[0])

            def f(ap):
                return ap.bitcast(F32)

            def split_lo(i):
                dve.wait_ge(w_hi, i + 1)
                dve.tensor_tensor(wlo[i % RING][:], raw[i % RING][:], f(whi[i % RING][:]), ALU.subtract)\
                   .then_inc(w_lo, 1)

            def x_lo(hf):
                cols = slice(hf * HT, (hf + 1) * HT)
                dve.wait_ge(xf_hi_done, hf + 1)
                dve.tensor_tensor(xf_lo[:, :, cols], x_f[:, :, cols], f(xf_hi[:, :, cols]), ALU.subtract)\
                   .then_inc(xf_lo_done, 1)

            def v_scale(g, t):
                r = rows(t)
                dve.wait_ge(v_mm, TILES * g + t + 1)
                if g and t == 0:
                    dve.wait_ge(y_mm, 4)
                dve.scalar_tensor_tensor(v_tok[0:r, t, :], bank[0:r, 4 + (TILES * g + t) % 4, :],
                                         scale_col[0:r, t:t + 1], v_bias[0:r, g * 512:(g + 1) * 512],
                                         ALU.mult, ALU.add).then_inc(v_biased, 1)

            def u_scale(g, n):
                j, hf = n // 2, n % 2
                cols = slice(hf * HT, (hf + 1) * HT)
                dve.wait_ge(u_mm, 8 * g + n + 1)
                if g:
                    dve.wait_ge(y_lo, j + 1)
                dve.tensor_tensor(u_feat[:, j, cols], bank[:, n % 4, 0:HT], scale_row[:, cols], ALU.mult)\
                   .then_inc(u_scaled, 1)

            def gate(g, j):
                hi, lo = (gated1_hi, gated1_lo) if g else (gated0_hi, gated0_lo)
                a = 6 if j % 2 == 0 else 4
                dve.wait_ge(y_mm, 4 * g + j + 1)
                dve.wait_ge(u_act, 8 * g + 2 * j + 2)
                for b_, c0 in ((a, 0), (a + 1, 512)):
                    u = u_feat[:, j, c0:min(c0 + 512, T)]
                    ins = dve.tensor_tensor(u, bank[:, b_, 0:u.shape[1]], u, ALU.mult)
                ins.then_inc(y_gated, 1)
                dve.wait_ge(y_hi, 4 * g + j + 1)
                dve.tensor_tensor(lo[:, j, :], u_feat[:, j, :], f(hi[:, j, :]), ALU.subtract).then_inc(y_lo, 1)

            x_lo(0)
            split_lo(V0)
            x_lo(1)
            dve.wait_ge(rms_done, 1)
            link(dve.tensor_scalar(scale_col[:], scale_col[:], 1e-8, None, ALU.add))
            link(dve.reciprocal(scale_col[:], scale_col[:]))
            dve.wait_ge(consts, 15)
            for t in range(TILES):
                r = rows(t)
                ins = dve.tensor_scalar(diag[:, t * P:t * P + r], ident[:, 0:r], scale_col[:, t:t + 1], None, ALU.mult)
            ins.then_inc(diag_done, 1)
            dve.wait_ge(small_in, 96)
            v_scale(0, 0)
            v_scale(0, 1)
            split_lo(U0)
            for t in range(2, 5):
                v_scale(0, t)
            split_lo(U1)
            v_scale(0, 5)
            v_scale(0, 6)
            split_lo(V1)
            dve.tensor_copy(ones_r[:], ones[:])
            dve.tensor_copy(before_r[:], before[:])
            link(dve.tensor_reduce(same_b[:], ident[:].rearrange("p (b i) -> p b i", i=N), AX, ALU.add))
            dve.tensor_tensor(mix[:].rearrange("p h (b i) -> p h b i", i=N),
                              bc(taps[:].rearrange("p (h i) -> p h i", i=N).unsqueeze(2), [P, MH, BS, N]),
                              bc(same_b[:].unsqueeze(1).unsqueeze(3), [P, MH, BS, N]), ALU.mult)\
                .then_inc(mix_done, 1)
            dve.wait_ge(scale_row_done, 2)
            for n in range(8):
                u_scale(0, n)
            gate(0, 0)
            for j in range(4):
                if j < 3:
                    gate(0, j + 1)
                u_scale(1, 2 * j)
                u_scale(1, 2 * j + 1)
                if j in (0, 2):
                    split_lo(O1 if j else O0)
            split_lo(WK)
            for t in range(TILES):
                v_scale(1, t)
            split_lo(CTX0)
            for j in range(4):
                gate(1, j)

            def norm_stats(t, var):
                r, b = rows(t), t % 2
                link(dve.bn_stats(bn[0:r, b, :], x[0:r, t, :]))
                dve.bn_aggr(mv[0:r, b, :], bn[0:r, b, :]).then_inc(var, 1)

            def norm_apply(t, std_done, done):
                r, b = rows(t), t % 2
                dve.wait_ge(std_done, t + 1)
                link(dve.reciprocal(rstd[0:r, b:b + 1], std[0:r, b:b + 1]))
                dve.tensor_scalar(x[0:r, t, :], x[0:r, t, :], mv[0:r, b, 0:1], rstd[0:r, b:b + 1],
                                  ALU.subtract, ALU.mult).then_inc(done, 1)

            def norm_factors(t, std_done, applied, ready):
                r, b = rows(t), t % 2
                dve.wait_ge(std_done, t + 1)
                if t >= 2:
                    dve.wait_ge(applied, t - 1)
                link(dve.reciprocal(rstd[0:r, b:b + 1], std[0:r, b:b + 1]))
                dve.scalar_tensor_tensor(shift[0:r, b:b + 1], mv[0:r, b, 0:1], -1.0, rstd[0:r, b:b + 1],
                                         ALU.mult, ALU.mult).then_inc(ready, 1)

            dve.wait_ge(res1, 4)
            for t in range(TILES):
                r = rows(t)
                dve.wait_ge(o_mm, t + 1)
                dve.tensor_tensor(x[0:r, t, :], bank[0:r, t % 4, :], x[0:r, t, :], ALU.add).then_inc(r1_done, 1)
                dve.wait_ge(r1_done, t + 1)
                norm_stats(t, var1)
                if t:
                    norm_apply(t - 1, std1, x1_done)
            norm_apply(TILES - 1, std1, x1_done)
            split_lo(CTX1)
            for t in range(TILES):
                if t == 4:
                    split_lo(WQ)
                r = rows(t)
                dve.wait_ge(x1t_hi, t + 1)
                dve.tensor_tensor(x1_lo[:, :, t * P:t * P + r],
                                  bank[:, 4 + t % 2, :].rearrange("p (k c) -> p k c", k=KD)[:, :, 0:r],
                                  f(x1_hi[:, :, t * P:t * P + r]), ALU.subtract).then_inc(x1t_lo, 1)
            split_lo(WV)
            dve.wait_ge(bias2_in, 16)

            def values_biased(n):
                dve.wait_ge(va_mm, n + 1)
                if n >= 2:
                    dve.wait_ge(pv_mm, n - 1)
                dve.tensor_tensor(v_att[:, n % 2, :], bank[0:L, 6, :], att_bias[0:L, 0, :], ALU.add)\
                   .then_inc(va_done, 1)

            def scores_masked(n, r):
                dve.wait_ge(s_mm, 2 * n + r + 1)
                if n >= 2:
                    dve.wait_ge(pt_mm, 2 * n + r - 3)
                s = probs[:, n % 2, r * HB:(r + 1) * HB].rearrange("l (j g s) -> l j g s", j=2, g=G4)
                dve.tensor_tensor(s, bank[0:L, 2 * r:2 * r + 2, 0:G4 * L].rearrange("l j (g s) -> l j g s", g=G4),
                                  bc(causal[:].unsqueeze(1).unsqueeze(1), [L, 2, G4, L]), ALU.add)\
                   .then_inc(s_read, 1)

            def scores_max(n, r):
                dve.wait_ge(s_read, 2 * n + r + 1)
                dve.tensor_reduce(row_max[:, n % 2, 8 * r:8 * r + 8], heads8(probs, n, r), AX, ALU.max)\
                   .then_inc(s_max, 1)

            def normalised(n, r):
                total = row_sum[:, n % 2, 8 * r:8 * r + 8]
                dve.wait_ge(s_exp, 2 * n + r + 1)
                link(dve.tensor_reduce(total, heads8(probs, n, r), AX, ALU.add))
                if r:
                    dve.reciprocal(total, total).then_inc(s_total, 1)
                else:
                    link(dve.reciprocal(total, total))
                    dve.tensor_tensor(heads8(probs, n, r), heads8(probs, n, r), bc(total.unsqueeze(2), [L, 8, L]),
                                      ALU.mult).then_inc(s_norm[0], 1)

            def attended_lo(n):
                dve.wait_ge(at_hi, n + 1)
                mine = lambda a: a[:].rearrange("p k (l n) -> p k l n", n=N)[:, :, :, n]
                dve.tensor_tensor(mine(att_lo), bank[:, 7, 0:KD * L].rearrange("p (k c) -> p k c", k=KD),
                                  f(mine(att_hi)), ALU.subtract).then_inc(at_lo, 1)

            scores_masked(0, 0)
            scores_max(0, 0)
            scores_masked(0, 1)
            scores_max(0, 1)
            values_biased(0)
            scores_masked(1, 0)
            normalised(0, 0)
            normalised(0, 1)
            scores_masked(1, 1)
            scores_max(1, 0)
            scores_max(1, 1)
            values_biased(1)
            normalised(1, 0)
            normalised(1, 1)
            for n in range(N):
                if n + 2 < N:
                    scores_masked(n + 2, 0)
                    scores_max(n + 2, 0)
                    scores_masked(n + 2, 1)
                    scores_max(n + 2, 1)
                attended_lo(n)
                if n + 2 < N:
                    normalised(n + 2, 0)
                    values_biased(n + 2)
                    normalised(n + 2, 1)
            dve.wait_ge(res2, 2)
            for t in range(TILES):
                r = rows(t)
                dve.wait_ge(o2_mm, t + 1)
                ins = dve.tensor_tensor(x[0:r, t, :], bank[0:r, t % 4, :], x[0:r, t, :], ALU.add)
                ins.then_inc(r2_done, 1)
                dve.wait_ge(r2_done, t + 1)
                norm_stats(t, var2)
                if t:
                    norm_factors(t - 1, std2, x2_done, norm2)
            norm_factors(TILES - 1, std2, x2_done, norm2)

            link(dve.memset(logits[:], 0.0))
            dve.tensor_copy(sel[:, TILES, :], zeros[:, 0:E])
            dve.wait_ge(lg_mm, TILES)
            lg = bank[:, 7, 0:TILES * E].rearrange("p (t e) -> p t e", e=E)
            dve.tensor_copy(logits[:, 0:FULL, :], lg[:, 0:FULL, :])
            link(dve.tensor_copy(logits[0:LAST, FULL:, :], lg[0:LAST, FULL:, :]))
            col = lambda a, s=S3: bc(a[:].unsqueeze(2), s)
            link(dve.tensor_reduce(r_col[:], logits[:], AX, ALU.max))
            dve.tensor_tensor(t_a[:], logits[:], col(r_col), ALU.subtract).then_inc(lg_shift, 1)
            dve.wait_ge(lg_exped, 1)
            mine = bc(lg_exp[:].unsqueeze(3), [P, TILES, E, E])
            other = bc(lg_exp[:].unsqueeze(2), [P, TILES, E, E])
            gt4, eq4 = (a[:].rearrange("p t (e o) -> p t e o", e=E) for a in (gt, eq))
            link(dve.tensor_tensor(eq4, other, mine, ALU.is_equal))
            dve.tensor_tensor(gt4, other, mine, ALU.is_gt)
            link(dve.tensor_tensor(eq[:], eq[:], bc(lower[:].rearrange("p e o -> p (e o)").unsqueeze(1),
                                                    [P, TILES, E * E]), ALU.mult))
            link(dve.tensor_tensor(gt[:], gt[:], eq[:], ALU.add))
            link(dve.tensor_reduce(rank[:], gt4, AX, ALU.add))
            dve.scalar_tensor_tensor(sel[:, 0:TILES, :], rank[:], 1.5, bc(valid[:], S3), ALU.is_lt, ALU.mult)\
               .then_inc(sel_done, 1)
            dve.tensor_scalar(pick1[:], rank[:], 0.0, None, ALU.is_equal)
            link(dve.tensor_scalar(pick2[:], rank[:], 1.0, None, ALU.is_equal))
            dve.wait_ge(rank_mm, 1)
            places = bank[:, 5, 0:(TILES + 1) * E].rearrange("p (t e) -> p t e", e=E)
            link(dve.scalar_tensor_tensor(place0[:], places[:, 0:TILES, 0], 1.0, f(sel[:, 0:TILES, 0]),
                                          ALU.add, ALU.mult))
            for t in range(TILES):
                dve.tensor_scalar(slot0[:, t, :], slots[:], place0[:, t:t + 1], None, ALU.is_equal)\
                   .then_inc(slot_done, 1)
            link(dve.tensor_reduce(m_col[:, 0:1], places[:, TILES, :], AX, ALU.max))
            link(dve.tensor_scalar(m_col[:, 1:2], m_col[:, 0:1], float(CAP), None, ALU.is_gt))
            dve.tensor_scalar(n_blocks[:], m_col[:, 1:2], float(BLOCKS - E), float(E), ALU.mult, ALU.add)\
               .then_inc(blocks_ready, 1)
            dve.tensor_scalar(over[:], places[:, 0:TILES, :], float(CAP), None, ALU.is_ge)
            link(dve.tensor_tensor(place[:], places[:, 0:TILES, :], bc(first_row[:].unsqueeze(1), S3), ALU.add))
            for c in range(2, PASSES):
                link(dve.scalar_tensor_tensor(over[:], places[:, 0:TILES, :], float(c * CAP), over[:],
                                              ALU.is_ge, ALU.add))
            link(dve.scalar_tensor_tensor(place[:], over[:], float((E - 1) * CAP), place[:], ALU.mult, ALU.add))
            dve.tensor_tensor(over[:], place[:], pick1[:], ALU.mult)
            link(dve.tensor_tensor(over2[:], place[:], pick2[:], ALU.mult))
            with nc.allow_low_precision("whole numbers"):
                dve.tensor_reduce(row1[:], over[:], AX, ALU.add)
                dve.tensor_reduce(row2[:], over2[:], AX, ALU.add).then_inc(rows_ready, 1)
            dve.wait_ge(rows_ready, 1)
            link(dve.tensor_reduce(r_col[:], lg_exp[:], AX, ALU.add))
            link(dve.reciprocal(r_col2[:], r_col[:]))
            link(dve.tensor_tensor(prob[:], lg_exp[:], col(r_col2), ALU.mult))
            dve.tensor_tensor(over[:], pick1[:], prob[:], ALU.mult)
            link(dve.tensor_tensor(over2[:], pick2[:], prob[:], ALU.mult))
            dve.tensor_reduce(gate1[:], over[:], AX, ALU.add)
            link(dve.tensor_reduce(gate2[:], over2[:], AX, ALU.add))
            link(dve.tensor_tensor(r_col[:], gate1[:], gate2[:], ALU.add))
            link(dve.reciprocal(r_col2[:], r_col[:]))
            dve.tensor_tensor(gate1[:], gate1[:], r_col2[:], ALU.mult)
            link(dve.tensor_tensor(gate2[:], gate2[:], r_col2[:], ALU.mult))

            dve.wait_ge(w_lo, FIRST + 2)

            def expert_lo(g, j):
                i = FIRST + j
                dve.wait_ge(w_hi, g * PER + (i + 1))
                dve.tensor_tensor(wlo[i % RING][:], raw[i % RING][:], f(whi[i % RING][:]), ALU.subtract)\
                   .then_inc(w_lo, 1)

            def expert(g):
                first = isinstance(g, int)
                for b in range(2):
                    dve.wait_ge(xgt_hi, g * 2 + b + 1)
                    dve.tensor_tensor(xg_lo[:, 2 * b:2 * b + 2, :],
                                      bank[:, 6 + b, :].rearrange("p (k c) -> p k c", k=2),
                                      f(xg_hi[:, 2 * b:2 * b + 2, :]), ALU.subtract).then_inc(xgt_lo, 1)
                expert_lo(g, 2)
                expert_lo(g, 3)
                for q, ahead in ((0, (4,)), (1, (5, 6)), (2, (7, 8)), (3, (9,))):
                    half = q % 2
                    dve.wait_ge(h_act, g * 8 + 2 * q + 2)
                    if not first or q >= 2:
                        dve.wait_ge(g2_mm, g * 4 + (q - 1))
                    dve.tensor_copy(h_hi[:, half, :, :], hidden[:, half, :, :]).then_inc(h_split_hi, 1)
                    dve.wait_ge(h_split_hi, g * 4 + q + 1)
                    dve.tensor_tensor(h_lo[:, half, :, :], hidden[:, half, :, :], f(h_hi[:, half, :, :]),
                                      ALU.subtract).then_inc(h_split, 1)
                    for j in ahead:
                        expert_lo(g, j)

            expert(0)
            blocks = dve.value_load(n_blocks[0:1, 0:1], min_val=E, max_val=BLOCKS)
            with dve.Fori(1, blocks) as g:
                expert(g)

            def step(ins):
                steps[0] += 1
                ins.then_inc(dve_step, 1)
                return steps[0]

            def add_share(t, c, gate, after=None):
                r = rows(t)
                dve.wait_ge(pick_in[t][c], 16)
                if after:
                    dve.wait_ge(dve_step, after)
                return step(dve.scalar_tensor_tensor(x[0:r, t, :], picked[0:r, t, c, :], gate[0:r, t:t + 1],
                                                     x[0:r, t, :], ALU.mult, ALU.add))

            stats = None
            for t in range(TILES + 1):
                if t < TILES:
                    share = add_share(t, 0, gate1)
                if t:
                    q, rq = (t - 1) % 2, rows(t - 1)
                    dve.wait_ge(dve_step, stats)
                    dve.bn_aggr(mv[0:rq, q, :], bn[0:rq, q, :]).then_inc(var3, 1)
                if t < TILES:
                    share = add_share(t, 1, gate2, share)
                if t:
                    dve.wait_ge(std3, t)
                    if t >= 3:
                        dve.wait_ge(out_ready, t - 2)
                    inverse = step(dve.reciprocal(rstd[0:rq, q:q + 1], std[0:rq, q:q + 1]))
                if t < TILES:
                    dve.wait_ge(dve_step, share)
                    stats = step(dve.bn_stats(bn[0:rows(t), t % 2, :], x[0:rows(t), t, :]))
                if t:
                    dve.wait_ge(dve_step, inverse)
                    dve.scalar_tensor_tensor(shift[0:rq, q:q + 1], mv[0:rq, q, 0:1], -1.0, rstd[0:rq, q:q + 1],
                                             ALU.mult, ALU.mult).then_inc(norm3, 1)

        @block.tensor
        def _(pe):
            def wh(i, sub=512):
                return (whi[i % RING][:, 0:KD * sub].rearrange("p (k n) -> p k n", k=KD),
                        wlo[i % RING][:, 0:KD * sub].rearrange("p (k n) -> p k n", k=KD))

            def mm3(o, a, b, first, last):
                pe.matmul(o, a[0], b[0], start=first, stop=False)
                pe.matmul(o, a[0], b[1], start=False, stop=False)
                return pe.matmul(o, a[1], b[0], start=False, stop=last)

            xf = (xf_hi, xf_lo)

            def v_tile(g, t):
                idx, r = TILES * g + t, rows(t)
                if idx >= 4:
                    pe.wait_ge(v_biased, idx - 3)
                if g and t == 0:
                    pe.wait_ge(y_gated, 4)
                w = wh(V1 if g else V0)
                for k in range(KD):
                    mm = mm3(bank[0:r, 4 + idx % 4, :], [a[:, k, t * P:t * P + r] for a in xf],
                             [a[:, k, :] for a in w], k == 0, k == KD - 1)
                mm.then_inc(v_mm, 1)

            def u_half(g, n):
                j, hf = n // 2, n % 2
                if 8 * g + n >= 4:
                    pe.wait_ge(u_scaled, 8 * g + n - 3)
                w = wh(U1 if g else U0)
                for k in range(KD):
                    mm = mm3(bank[:, n % 4, 0:HT], [a[:, k, j * P:(j + 1) * P] for a in w],
                             [a[:, k, hf * HT:(hf + 1) * HT] for a in xf], k == 0, k == KD - 1)
                mm.then_inc(u_mm, 1)

            def mix_head(g, j):
                idx = 4 * g + j
                if idx >= 2:
                    pe.wait_ge(y_gated, idx - 1)
                a = 6 if j % 2 == 0 else 4
                for t in range(TILES):
                    r = rows(t)
                    mm = pe.matmul(bank[:, a + t // 4, (t % 4) * P:(t % 4) * P + r],
                                   v_tok[0:r, t, j * P:(j + 1) * P], mix[0:r, 4 * g + j, 0:r],
                                   start=True, stop=True)
                mm.then_inc(y_mm, 1)

            gated = [(gated0_hi, gated0_lo), (gated1_hi, gated1_lo)]

            def project(t, half):
                r = rows(t)
                if half == 0 and t >= 4:
                    pe.wait_ge(r1_done, t - 3)
                w = wh(O1 if half else O0)
                for k in range(KD):
                    mm = mm3(bank[0:r, t % 4, :], [a[:, k, t * P:t * P + r] for a in gated[half]],
                             [a[:, k, :] for a in w], half == 0 and k == 0, half == 1 and k == KD - 1)
                if half:
                    mm.then_inc(o_mm, 1)

            pe.wait_ge(xf_lo_done, 1)
            pe.wait_ge(w_hi, V0 + 1)
            w_hi0, w_lo0 = wh(V0)
            EARLY = HT // P
            for t in range(EARLY):
                for k in range(KD):
                    for i, a in enumerate(xf):
                        pe.matmul(bank[:, 4 + t, :], a[:, k, t * P:(t + 1) * P], w_hi0[:, k, :],
                                  start=(k == 0 and i == 0), stop=False)
            pe.wait_ge(w_lo, V0 + 1)
            for t in range(EARLY):
                for k in range(KD):
                    mm = pe.matmul(bank[:, 4 + t, :], xf_hi[:, k, t * P:(t + 1) * P], w_lo0[:, k, :],
                                   start=False, stop=(k == KD - 1))
                mm.then_inc(v_mm, 1)
            pe.wait_ge(xf_lo_done, 2)
            for t in range(EARLY, TILES):
                v_tile(0, t)
            pe.wait_ge(diag_done, 1)
            for hf in range(2):
                mm = pe.matmul(bank[:, 2 + hf, 0:HT], ones[:], diag[:, hf * HT:(hf + 1) * HT], start=True, stop=True)
                mm.then_inc(scale_mm, 1)
            pe.wait_ge(w_lo, U0 + 1)
            u_half(0, 0)
            u_half(0, 1)
            pe.wait_ge(scale_row_done, 2)
            for n in range(2, 8):
                u_half(0, n)
            pe.wait_ge(mix_done, 1)
            pe.wait_ge(v_act, TILES)
            mix_head(0, 0)
            mix_head(0, 1)
            pe.wait_ge(w_lo, U1 + 1)
            for j in range(4):
                u_half(1, 2 * j)
                u_half(1, 2 * j + 1)
                if j < 2:
                    mix_head(0, j + 2)
            pe.wait_ge(w_lo, V1 + 1)
            for t in range(TILES):
                v_tile(1, t)
            pe.wait_ge(y_lo, 4)
            pe.wait_ge(w_lo, O0 + 1)
            pe.wait_ge(u_scaled, 16)
            project(0, 0)
            pe.wait_ge(v_act, 2 * TILES)
            mix_head(1, 0)
            mix_head(1, 1)
            project(1, 0)
            mix_head(1, 2)
            project(2, 0)
            mix_head(1, 3)
            project(3, 0)
            pe.wait_ge(y_lo, 8)
            pe.wait_ge(w_lo, O1 + 1)
            for t in range(4):
                project(t, 1)
            for t in range(4, TILES):
                project(t, 0)
                project(t, 1)

            def kq(i, w, src):
                n = i % 8
                j = n % 4
                if i >= 2:
                    pe.wait_ge(kq_done, i - 1)
                for k in range(KD):
                    mm = mm3(bank[:, 6 + i % 2, 0:HT], [a[:, k, j * P:(j + 1) * P] for a in w],
                             [a[:, k, :] for a in src], k == 0, k == KD - 1)
                mm.then_inc(kq_mm, 1)

            ctx = [wh(CTX0, HT), wh(CTX1, HT)]
            ctx_piece = lambda i: CTX1 if i >= 4 else CTX0
            def x1_transpose(t):
                r = rows(t)
                pe.wait_ge(x1_done, t + 1)
                if t >= 2:
                    pe.wait_ge(x1t_lo, t - 1)
                for k in range(KD):
                    mm = pe.transpose(bank[:, 4 + t % 2, k * P:k * P + r], x[0:r, t, k * P:(k + 1) * P],
                                      ident[0:r, 0:r])
                mm.then_inc(x1t_mm, 1)

            for i in range(8):
                pe.wait_ge(w_lo, ctx_piece(i) + 1)
                kq(i, wh(WK), ctx[i // 4])
                if i < TILES:
                    x1_transpose(i)
            pe.wait_ge(x1t_lo, TILES)
            pe.wait_ge(w_lo, WQ + 1)
            for hf in range(2):
                for j in range(4):
                    kq(8 + 4 * hf + j, wh(WQ), [a[:, :, hf * HT:(hf + 1) * HT] for a in (x1_hi, x1_lo)])

            pe.wait_ge(w_lo, WV + 1)
            pe.wait_ge(kq_done, 16)

            def values(n):
                if n >= 1:
                    pe.wait_ge(va_done, n)
                if n >= 2:
                    pe.wait_ge(pv_mm, n - 1)
                c0 = (n % 4) * L
                for k in range(KD):
                    mm = mm3(bank[0:L, 6, :], [a[:, k, c0:c0 + L] for a in ctx[n // 4]],
                             [a[:, k, :] for a in wh(WV)], k == 0, k == KD - 1)
                mm.then_inc(va_mm, 1)

            def scores(n):
                cols = slice(n * L, (n + 1) * L)
                for r in range(2):
                    if n >= 1:
                        pe.wait_ge(s_read, 2 * n + r - 1)
                    for g in range(G4):
                        for j in range(2 * r, 2 * r + 2):
                            part = slice(AD * j, AD * (j + 1))
                            mm = pe.matmul(bank[0:L, j, g * L:(g + 1) * L], q_feat[part, g, cols],
                                           k_feat[part, g, cols], start=True, stop=True)
                    mm.then_inc(s_mm, 1)

            def probs_turned(n, r):
                pe.wait_ge(s_norm[r], n + 1)
                if 2 * n + r:
                    pe.wait_ge(pt_done, 2 * n + r)
                for jj in range(2):
                    for g in range(G4):
                        c = ((2 * r + jj) * G4 + g) * L
                        mm = pe.transpose(bank[0:L, 4 + jj, g * L:(g + 1) * L], probs[:, n % 2, c:c + L],
                                          ident[0:L, 0:L])
                mm.then_inc(pt_mm, 1)

            def weighted(n):
                pe.wait_ge(va_done, n + 1)
                pe.wait_ge(pt_done, 2 * n + 2)
                if n:
                    pe.wait_ge(at_lo, n)
                for r in range(2):
                    for jj in range(2):
                        j = 2 * r + jj
                        for g in range(G4):
                            h = 4 * g + j
                            c = (jj * G4 + g) * L
                            mm = pe.matmul(bank[AD * j:AD * (j + 1), 7, g * L:(g + 1) * L],
                                           v_att[:, n % 2, h * AD:(h + 1) * AD], probs_t[:, n % 2, r, c:c + L],
                                           start=True, stop=True, tile_position=(0, AD * j))
                mm.then_inc(pv_mm, 1)

            scores(0)
            values(0)
            scores(1)
            values(1)
            for n in range(N):
                probs_turned(n, 0)
                if 0 < n < N - 1:
                    values(n + 1)
                probs_turned(n, 1)
                if n + 2 < N:
                    scores(n + 2)
                weighted(n)

            def x2_transpose(t):
                r = rows(t)
                pe.wait_ge(x2_done, t + 1)
                if t >= 2:
                    pe.wait_ge(x2t_done, t - 1)
                for k in range(KD):
                    mm = pe.transpose(bank[:, 4 + t % 2, k * P:k * P + r], x[0:r, t, k * P:(k + 1) * P],
                                      ident[0:r, 0:r])
                mm.then_inc(x2t_mm, 1)

            def route(t):
                r = rows(t)
                pe.wait_ge(x2t_done, t + 1)
                for k in range(KD):
                    mm = pe.matmul(bank[0:r, 7, t * E:(t + 1) * E], x2_feat[:, k, t * P:t * P + r], wr[:, k, :],
                                   start=(k == 0), stop=(k == KD - 1))
                mm.then_inc(lg_mm, 1)

            pe.wait_ge(at_lo, N)
            pe.wait_ge(w_lo, WO + 1)
            pe.wait_ge(s_read, 2 * N)
            pe.wait_ge(pt_done, 2 * N)
            for t in range(TILES):
                r = rows(t)
                if t >= 4:
                    pe.wait_ge(r2_done, t - 3)
                for k in range(KD):
                    mm = mm3(bank[0:r, t % 4, :], [a[:, k, t * P:t * P + r] for a in (att_hi, att_lo)],
                             [a[:, k, :] for a in wh(WO)], k == 0, k == KD - 1)
                mm.then_inc(o2_mm, 1)
                if t >= 3:
                    x2_transpose(t - 3)
                if t >= 4:
                    route(t - 4)
            for t in range(TILES - 3, TILES):
                x2_transpose(t)
                route(t - 1)
            route(TILES - 1)
            pe.wait_ge(sel_done, 1)
            mm = pe.matmul(bank[:, 5, 0:(TILES + 1) * E], before_r[:], sel[:].rearrange("p t e -> p (t e)"),
                           start=True, stop=False)
            for t in range(TILES):
                mm = pe.matmul(bank[:, 5, (t + 1) * E:(TILES + 1) * E], ones_r[:],
                               bc(sel[:, t:t + 1, :], [P, TILES - t, E]), start=False, stop=(t == TILES - 1))
            mm.then_inc(rank_mm, 1)

            def through_w1(g, q):
                i = FIRST + W1_PIECE[q]
                pe.wait_ge(w_lo, g * PER + (i + 1))
                w = wh(i)
                for ft in range(4):
                    b = ft // 2
                    if b * 2 == ft and (q >= 2 or not isinstance(g, int)):
                        pe.wait_ge(h_act, g * 8 + (2 * q + b - 3))
                    for k in range(KD):
                        if (q, ft, k) == (0, 0, 2):
                            pe.wait_ge(xgt_lo, g * 2 + 2)
                        mm = mm3(bank[:, 2 * (q % 2) + b, (ft % 2) * CAP:(ft % 2 + 1) * CAP],
                                 [a[:, k, ft * P:(ft + 1) * P] for a in w],
                                 [a[:, k, :] for a in (xg_hi, xg_lo)], k == 0, k == KD - 1)
                    if ft % 2:
                        mm.then_inc(g1_mm, 1)

            def through_w2(g, q, back=0):
                i = FIRST + W2_PIECE[q] - PER * back
                pe.wait_ge(w_lo, g * PER + (i + 1))
                pe.wait_ge(h_split, g * 4 + (q + 1 - 4 * back))
                if q == 0 and isinstance(g, int):
                    pe.wait_ge(rows_ready, 1)
                elif q == 0:
                    pe.wait_ge(y_read, g)
                w = wh(FIRST + W2_PIECE[q])
                for s in range(CT):
                    for ft in range(4):
                        mm = mm3(bank[:, 4 + s, :], [a[:, q % 2, ft, s * P:(s + 1) * P] for a in (h_hi, h_lo)],
                                 [a[:, ft, :] for a in w], q == 0 and ft == 0, q == 3 and ft == 3)
                mm.then_inc(g2_mm, 1)

            def select_block0():
                pe.wait_ge(x2_lo_done, TILES)
                for b in range(2):
                    for k in range(2 * b, 2 * b + 2):
                        for t in range(TILES):
                            if k == 0:
                                pe.wait_ge(slot_done, t + 1)
                            for i, a in enumerate((x2_hi, x2_lo)):
                                mm = pe.matmul(bank[:, 6 + b, (k % 2) * CAP:(k % 2 + 1) * CAP],
                                               a[0:rows(t), t, k * P:(k + 1) * P], slot0[0:rows(t), t, :],
                                               start=(t == 0 and i == 0), stop=(t == TILES - 1 and i == 1))
                    mm.then_inc(xgt_mm, 1)

            def expert(g):
                if isinstance(g, int):
                    select_block0()
                else:
                    pe.wait_ge(xg_in, g * 16)
                    for b in range(2):
                        pe.wait_ge(xgt_lo, g * 2 + (b - 1))
                        for k in range(2 * b, 2 * b + 2):
                            for s in range(CT):
                                c = (k % 2) * CAP + s * P
                                mm = pe.transpose(bank[:, 6 + b, c:c + P], xg[:, s, k * P:(k + 1) * P], ident[:])
                        mm.then_inc(xgt_mm, 1)
                    through_w2(g, 3, back=1)
                pe.wait_ge(xgt_lo, g * 2 + 1)
                through_w1(g, 0)
                through_w1(g, 1)
                through_w2(g, 0)
                through_w1(g, 2)
                through_w2(g, 1)
                through_w1(g, 3)
                through_w2(g, 2)

            expert(0)
            blocks = pe.value_load(n_blocks[0:1, 0:1], min_val=E, max_val=BLOCKS)
            with pe.Fori(1, blocks) as g:
                expert(g)
            through_w2(blocks, 3, back=1)


def kernel(x, ctx_1024, L0_attn_key, L0_attn_value, L0_attn_u_w, L0_attn_u_b, L0_attn_v_w, L0_attn_v_b,
           L0_attn_o_w, L0_attn_o_b, L0_attn_pos, L0_attn_zero, L0_attn_neg, L0_xattn_Wq, L0_xattn_bq,
           L0_xattn_Wk, L0_xattn_bk, L0_xattn_Wv, L0_xattn_bv, L0_xattn_Wo, L0_xattn_bo, L0_ffn_W1,
           L0_ffn_W2, L0_ffn_Wr):
    import concourse.bacc as bacc
    from concourse.bass_utils import run_bass_kernel_spmd

    def by_k(m):
        return m.reshape(m.shape[0], -1, P).transpose(2, 1, 0)

    def piece(m):
        return by_k(m).reshape(P, -1)

    x = np.asarray(x)
    xt = x.transpose(1, 0, 2).reshape(T, D)
    u_w, v_w, o_w = np.asarray(L0_attn_u_w), np.asarray(L0_attn_v_w), np.asarray(L0_attn_o_w)
    ctx = np.asarray(ctx_1024)[:, :L].reshape(T, D)
    halves = [by_k(ctx[h * HT:(h + 1) * HT]).reshape(P, KD * HT) for h in range(2)]
    halves = [np.concatenate([h, h[:, :2048 - KD * HT]], 1) for h in halves]
    pieces = np.stack([
        piece(v_w[:512]), piece(u_w[:512]), piece(u_w[512:]), piece(v_w[512:]),
        piece(o_w[:, :512]), piece(o_w[:, 512:]), piece(np.asarray(L0_xattn_Wk)), *halves,
        piece(np.asarray(L0_xattn_Wq)), piece(np.asarray(L0_xattn_Wv)), piece(np.asarray(L0_xattn_Wo))])
    w1 = np.asarray(L0_ffn_W1).reshape(E, 4, 512, KD, P).transpose(0, 1, 4, 3, 2).reshape(E, 4, P, 2048)
    w2 = np.asarray(L0_ffn_W2).reshape(E, D, 4, 4, P).transpose(0, 2, 4, 3, 1).reshape(E, 4, P, 2048)
    ffn = np.stack([(w1 if which == 1 else w2)[:, q] for which, q in ORDER], 1).reshape(E * PER, P, 2048)
    ffn = np.concatenate([ffn, ffn[:EXTRA]], 0)
    a = np.concatenate([np.asarray(L0_attn_neg)[:, :N - 1][:, ::-1], np.asarray(L0_attn_zero),
                        np.asarray(L0_attn_pos)[:, :N - 1]], 1)
    taps = np.tile(np.stack([a[:, N - 1 - j:2 * N - 1 - j] for j in range(N)]).reshape(N, MH * N), (BS, 1))

    def col(b):
        return np.asarray(b).reshape(-1, P).T

    arrays = {
        "x_tok": xt, "x_feat": by_k(xt), "pieces": pieces, "ffn_pieces": ffn,
        "u_b": col(L0_attn_u_b), "v_b": np.asarray(L0_attn_v_b), "o_b": np.asarray(L0_attn_o_b),
        "mix_taps": taps, "bq": col(L0_xattn_bq), "bk": col(L0_xattn_bk),
        "bv_bo": np.stack([np.asarray(L0_xattn_bv), np.asarray(L0_xattn_bo)]),
        "router_w": by_k(np.asarray(L0_ffn_Wr)),
    }
    arrays = {f"in_{k}": np.ascontiguousarray(v) for k, v in arrays.items()}
    nc = bacc.Bacc("TRN2", target_bir_lowering=False, num_devices=1)
    args = [nc.dram_tensor(k, v.shape, F32, kind="ExternalInput").ap() for k, v in arrays.items()]
    out = nc.dram_tensor("out", (T, D), F32, kind="ExternalOutput").ap()
    decoder_layer(nc, *args, out)
    result = run_bass_kernel_spmd(nc, [arrays], core_ids=[0])
    return result.results[0]["out"].reshape(L, N, D).transpose(1, 0, 2)
```
